# Optimizing a Trainium2 kernel written in Bass

```python
import numpy as np
import jax
import jax.numpy as jnp

def _softmax(x, axis=-1):
    return jax.nn.softmax(x, axis=axis)

def _gelu(x):
    return jax.nn.gelu(x, approximate=True)

def _silu(x):
    return jax.nn.silu(x)

def _sigmoid(x):
    return jax.nn.sigmoid(x)

def _layernorm(x, axis=-1, eps=1e-05):
    m = jnp.mean(x, axis=axis, keepdims=True)
    v = jnp.var(x, axis=axis, keepdims=True)
    return (x - m) / jnp.sqrt(v + eps)

def _scatter_add(tgt, idx, src, axis=0):
    return tgt.at[idx].add(src)

def _segment_sum(src, seg, n):
    return jax.ops.segment_sum(src, seg, n)
kernel_name = 'mk_seq_postln_d1_jaxref_r8_0e5d3e'

def setup_inputs(seed: int=0):
    np.random.seed(seed)
    _w = jnp.asarray

    def _L0_attn_setup():
        import jax, jax.numpy as jnp
        import numpy as np
        D_MODEL = 128
        N_HEADS = 16
        LATENT_HEADS = 8
        LATENT_DIM = 64
        N_LATENTS = 64
        WINDOW = 32
        HEAD_DIM = D_MODEL // N_HEADS
        LAT_HD = LATENT_DIM // LATENT_HEADS
        B, S = (2, 512)

        def _pool_to_latents(x):
            Bx, Sx, C = x.shape
            chunk = max(1, Sx // N_LATENTS)
            return x.reshape(Bx, N_LATENTS, chunk, C).mean(axis=2)

        def _local_window_attn(Q, K, V):
            Bx, H, Sx, D = Q.shape
            W = WINDOW
            nb = Sx // W
            Qb = Q.reshape(Bx, H, nb, W, D)
            Kp = jnp.pad(K, ((0, 0), (0, 0), (W, 0), (0, 0))).reshape(Bx, H, nb + 1, W, D)
            Vp = jnp.pad(V, ((0, 0), (0, 0), (W, 0), (0, 0))).reshape(Bx, H, nb + 1, W, D)
            Kw = jnp.concatenate([Kp[:, :, :-1], Kp[:, :, 1:]], axis=3)
            Vw = jnp.concatenate([Vp[:, :, :-1], Vp[:, :, 1:]], axis=3)
            i = jnp.arange(W)[:, None]
            j = jnp.arange(2 * W)[None, :]
            base = (j > i) & (j <= i + W)
            blk0 = (jnp.arange(nb) > 0)[:, None, None] | (j >= W)[None, :, :]
            mask = base[None, :, :] & blk0
            sc = jnp.einsum('bhnid,bhnjd->bhnij', Qb, Kw) / np.sqrt(D).astype(np.float32)
            sc = jnp.where(mask[None, None], sc, -jnp.inf)
            p = jax.nn.softmax(sc, axis=-1)
            out = jnp.einsum('bhnij,bhnjd->bhnid', p, Vw)
            return out.reshape(Bx, H, Sx, D)
        key = jax.random.key(seed)
        ks = jax.random.split(key, 11)
        std = 0.02
        w = lambda k, shp: jax.random.normal(k, shp, jnp.float32) * std
        return {'x': jax.random.normal(ks[0], (B, S, D_MODEL), jnp.float32), 'wq': w(ks[1], (D_MODEL, D_MODEL)), 'wk': w(ks[2], (D_MODEL, D_MODEL)), 'wv': w(ks[3], (D_MODEL, D_MODEL)), 'wgq': w(ks[4], (D_MODEL, LATENT_DIM)), 'wgk': w(ks[5], (D_MODEL, LATENT_DIM)), 'wgv': w(ks[6], (D_MODEL, LATENT_DIM)), 'r_out_w': w(ks[7], (LATENT_DIM, D_MODEL)), 'gate_local_w': w(ks[8], (N_HEADS, HEAD_DIM)), 'gate_remote_w': w(ks[9], (N_HEADS, HEAD_DIM)), 'w_out': w(ks[10], (D_MODEL, D_MODEL))}
    _L0_attn_in = _L0_attn_setup()

    def _L0_ffn_setup():
        import jax, jax.numpy as jnp
        import numpy as np
        HIDDEN = 128
        NUM_EXPERTS = 8
        TOP_K = 2
        B, S = (2, 256)
        key = jax.random.key(seed)
        k1, k2, k3, k4, k5 = jax.random.split(key, 5)
        d, dff, E = (HIDDEN, 4 * HIDDEN, NUM_EXPERTS)
        x = jax.random.normal(k1, (B, S, d), dtype=jnp.float32)
        W1 = jax.random.normal(k2, (E, d, dff), dtype=jnp.float32) * (1.0 / np.sqrt(d))
        b1 = jax.random.normal(k3, (E, dff), dtype=jnp.float32) * 0.01
        W2 = jax.random.normal(k4, (E, dff, d), dtype=jnp.float32) * (1.0 / np.sqrt(dff))
        b2 = jax.random.normal(k5, (E, d), dtype=jnp.float32) * 0.01
        return {'x': x, 'W1': W1, 'b1': b1, 'W2': W2, 'b2': b2}
    _L0_ffn_in = _L0_ffn_setup()
    _d = {'L0_attn_x': _L0_attn_in['x'], 'L0_attn_wq': _L0_attn_in['wq'], 'L0_attn_wk': _L0_attn_in['wk'], 'L0_attn_wv': _L0_attn_in['wv'], 'L0_attn_wgq': _L0_attn_in['wgq'], 'L0_attn_wgk': _L0_attn_in['wgk'], 'L0_attn_wgv': _L0_attn_in['wgv'], 'L0_attn_r_out_w': _L0_attn_in['r_out_w'], 'L0_attn_gate_local_w': _L0_attn_in['gate_local_w'], 'L0_attn_gate_remote_w': _L0_attn_in['gate_remote_w'], 'L0_attn_w_out': _L0_attn_in['w_out'], 'L0_ffn_W1': _L0_ffn_in['W1'], 'L0_ffn_b1': _L0_ffn_in['b1'], 'L0_ffn_W2': _L0_ffn_in['W2'], 'L0_ffn_b2': _L0_ffn_in['b2']}
    _x0 = _d['L0_attn_x']
    _d['L0_attn_x'] = jax.random.normal(jax.random.fold_in(jax.random.key(seed), 1), (4, 512, 128), dtype=_x0.dtype)
    del _x0
    return _d

def reference(L0_attn_x, L0_attn_wq, L0_attn_wk, L0_attn_wv, L0_attn_wgq, L0_attn_wgk, L0_attn_wgv, L0_attn_r_out_w, L0_attn_gate_local_w, L0_attn_gate_remote_w, L0_attn_w_out, L0_ffn_W1, L0_ffn_b1, L0_ffn_W2, L0_ffn_b2):

    def _L0_attn_ref(x, wq, wk, wv, wgq, wgk, wgv, r_out_w, gate_local_w, gate_remote_w, w_out):
        import jax, jax.numpy as jnp
        import numpy as np
        D_MODEL = 128
        N_HEADS = 16
        LATENT_HEADS = 8
        LATENT_DIM = 64
        N_LATENTS = 64
        WINDOW = 32
        HEAD_DIM = D_MODEL // N_HEADS
        LAT_HD = LATENT_DIM // LATENT_HEADS
        B, S = (2, 512)

        def _pool_to_latents(x):
            Bx, Sx, C = x.shape
            chunk = max(1, Sx // N_LATENTS)
            return x.reshape(Bx, N_LATENTS, chunk, C).mean(axis=2)

        def _local_window_attn(Q, K, V):
            Bx, H, Sx, D = Q.shape
            W = WINDOW
            nb = Sx // W
            Qb = Q.reshape(Bx, H, nb, W, D)
            Kp = jnp.pad(K, ((0, 0), (0, 0), (W, 0), (0, 0))).reshape(Bx, H, nb + 1, W, D)
            Vp = jnp.pad(V, ((0, 0), (0, 0), (W, 0), (0, 0))).reshape(Bx, H, nb + 1, W, D)
            Kw = jnp.concatenate([Kp[:, :, :-1], Kp[:, :, 1:]], axis=3)
            Vw = jnp.concatenate([Vp[:, :, :-1], Vp[:, :, 1:]], axis=3)
            i = jnp.arange(W)[:, None]
            j = jnp.arange(2 * W)[None, :]
            base = (j > i) & (j <= i + W)
            blk0 = (jnp.arange(nb) > 0)[:, None, None] | (j >= W)[None, :, :]
            mask = base[None, :, :] & blk0
            sc = jnp.einsum('bhnid,bhnjd->bhnij', Qb, Kw) / np.sqrt(D).astype(np.float32)
            sc = jnp.where(mask[None, None], sc, -jnp.inf)
            p = jax.nn.softmax(sc, axis=-1)
            out = jnp.einsum('bhnij,bhnjd->bhnid', p, Vw)
            return out.reshape(Bx, H, Sx, D)
        Bx, Sx, _ = x.shape
        chunk = max(1, Sx // N_LATENTS)
        Q = (x @ wq).reshape(Bx, Sx, N_HEADS, HEAD_DIM).transpose(0, 2, 1, 3)
        K = (x @ wk).reshape(Bx, Sx, N_HEADS, HEAD_DIM).transpose(0, 2, 1, 3)
        V = (x @ wv).reshape(Bx, Sx, N_HEADS, HEAD_DIM).transpose(0, 2, 1, 3)
        local = _local_window_attn(Q, K, V)
        GQ = (x @ wgq).reshape(Bx, Sx, LATENT_HEADS, LAT_HD).transpose(0, 2, 1, 3)
        GK = _pool_to_latents(x @ wgk).reshape(Bx, N_LATENTS, LATENT_HEADS, LAT_HD).transpose(0, 2, 1, 3)
        GV = _pool_to_latents(x @ wgv).reshape(Bx, N_LATENTS, LATENT_HEADS, LAT_HD).transpose(0, 2, 1, 3)
        lsc = jnp.einsum('bhsd,bhnd->bhsn', GQ, GK) / np.sqrt(LAT_HD).astype(np.float32)
        lmask = jnp.arange(N_LATENTS)[None, :] <= (jnp.arange(Sx) // chunk)[:, None]
        lsc = jnp.where(lmask[None, None], lsc, -jnp.inf)
        lp = jax.nn.softmax(lsc, axis=-1)
        rem = jnp.einsum('bhsn,bhnd->bhsd', lp, GV)
        rem = rem.transpose(0, 2, 1, 3).reshape(Bx, Sx, LATENT_DIM) @ r_out_w
        rem = rem.reshape(Bx, Sx, N_HEADS, HEAD_DIM).transpose(0, 2, 1, 3)
        gl = jax.nn.sigmoid(jnp.einsum('bhsd,hd->bhs', Q, gate_local_w))[..., None]
        gr = jax.nn.sigmoid(jnp.einsum('bhsd,hd->bhs', Q, gate_remote_w))[..., None]
        out = gl * local + gr * rem
        out = out.transpose(0, 2, 1, 3).reshape(Bx, Sx, D_MODEL)
        return out @ w_out

    def _L0_ffn_ref(x, W1, b1, W2, b2):
        import jax, jax.numpy as jnp
        import numpy as np
        HIDDEN = 128
        NUM_EXPERTS = 8
        TOP_K = 2
        B, S = (2, 256)
        Bm, Sm, d = x.shape
        E = W1.shape[0]
        x_flat = x.reshape(-1, d)
        h = jnp.mod(x_flat[:, :TOP_K].sum(axis=1).astype(jnp.int32), E)
        sel = jnp.stack([h, jnp.mod(h + 1, E)], axis=1)

        def step(acc, params):
            e, W1e, b1e, W2e, b2e = params
            w = jnp.any(sel == e, axis=1).astype(x.dtype) / TOP_K
            y = jnp.maximum(x_flat @ W1e + b1e, 0.0) @ W2e + b2e
            return (acc + w[:, None] * y, None)
        init = jnp.zeros_like(x_flat)
        out_flat, _ = jax.lax.scan(step, init, (jnp.arange(E), W1, b1, W2, b2))
        return out_flat.reshape(Bm, Sm, d)
    x = L0_attn_x
    x = _layernorm(x + _L0_attn_ref(x, L0_attn_wq, L0_attn_wk, L0_attn_wv, L0_attn_wgq, L0_attn_wgk, L0_attn_wgv, L0_attn_r_out_w, L0_attn_gate_local_w, L0_attn_gate_remote_w, L0_attn_w_out), axis=-1)
    x = _layernorm(x + _L0_ffn_ref(x, L0_ffn_W1, L0_ffn_b1, L0_ffn_W2, L0_ffn_b2), axis=-1)
    return x

_drawn_inputs = setup_inputs


def setup_inputs(seed=0):
    import zlib

    import numpy as np

    out = dict(_drawn_inputs(seed))
    spreads = {}
    factors = {'L0_attn_wq': 8.0,
     'L0_attn_wk': 7.371,
     'L0_attn_wv': 3.114,
     'L0_attn_wgq': 8.0,
     'L0_attn_wgk': 8.0,
     'L0_attn_wgv': 7.367,
     'L0_attn_r_out_w': 7.57,
     'L0_attn_gate_local_w': 8.0,
     'L0_attn_gate_remote_w': 8.0,
     'L0_attn_w_out': 2.752,
     'L0_ffn_b1': 8.0,
     'L0_ffn_b2': 8.0}
    for name, (base, spread) in spreads.items():
        noise = np.random.default_rng([zlib.crc32(name.encode()), seed]).standard_normal(out[name].shape)
        drawn = base * np.exp(spread * noise) if base else spread * noise
        out[name] = jnp.asarray(drawn.astype(out[name].dtype))
    for name, factor in factors.items():
        out[name] = (out[name] * factor).astype(out[name].dtype)
    return out
```

```python
from contextlib import ExitStack

import concourse.bass as bass
from concourse import mybir

ALU = mybir.AluOpType
ACT = mybir.ActivationFunctionType
AX = mybir.AxisListType
F32 = mybir.dt.float32
BF16 = mybir.dt.bfloat16
I32 = mybir.dt.int32
U32 = mybir.dt.uint32

P = 128
NEG = -1.0e30
ROUND = 12582912.0


def bass_windowed_latent_attention_hash_moe(
    nc, x, wq, wk, wv, wgq, wgk, wgv, r_out_w, gate_l, gate_r, w_out, W1, b1, W2, b2, out, seg,
):
    NB, S, D = x.shape
    H, HD = gate_l.shape
    LD = wgq.shape[1]
    LH = LD // HD
    W = 32
    NL = 64
    CH = S // NL
    E, _, F = W1.shape
    FC = F // P
    KT_ = S // P
    T = NB * KT_
    BLK = P // W
    HP = H // 2
    LP = LH // 2
    PW = 2 * HD + 2
    SCALE = float(HD) ** -0.5
    EPS = 1e-5
    SEG = seg.shape[0] // E
    XW = D + 1

    with ExitStack() as ctx:
        def sb(name, shape, dt=F32):
            return ctx.enter_context(nc.sbuf_tensor(name, shape, dt))

        def bank(name, dt=F32):
            return ctx.enter_context(nc.psum_tensor(name, [P, 512], dt))

        def sem(name):
            return ctx.enter_context(nc.semaphore(name))

        x_tok = sb("x_tok", [P, T, D])
        wq_s, wk_s, wv_s, wout_s = (sb(n, [P, P]) for n in ("wq_s", "wk_s", "wv_s", "wout_s"))
        wgq_s, wgk_s, wgv_s = (sb(n, [P, LD]) for n in ("wgq_s", "wgk_s", "wgv_s"))
        rout_s = sb("rout_s", [LD, P])
        gcol = sb("gcol", [P, 2])
        ident = sb("ident", [P, P])
        half = sb("half", [P, 2])
        blk16 = sb("blk16", [P, H])
        slot4 = sb("slot4", [P, 4])
        group4 = sb("group4", [P, 4])
        gmat = sb("gmat", [P, 2 * H])
        wv_par = sb("wv_par", [P, 2, P])
        wgv_par = sb("wgv_par", [P, 2, LD])
        sel_l = sb("sel_l", [2 * W, P], BF16)
        neg_l = sb("neg_l", [2 * W, 2 * W], BF16)
        sel_r = sb("sel_r", [P // CH, P], BF16)
        neg_r = sb("neg_r", [P // CH, KT_, NL], BF16)

        xT = sb("xT", [P, 2, W + S])
        KT = sb("KT", [P, 2, S])
        QT = sb("QT", [P, 2, S])
        Kx = sb("Kx", [P, 2, 4, W + S])
        Qg = sb("Qg", [P, 2, 4, S])
        xp = sb("xp", [P, 2, NL])
        GQT = sb("GQT", [LD, 2, S])
        GKs = sb("GKs", [LD, 2, NL])
        GKx = sb("GKx", [LD, 2, LH, NL])
        GVx = sb("GVx", [P, 2, LP, PW])
        gex = sb("gex", [P, 2, KT_, 2 * H])
        gat = sb("gat", [P, 2, KT_, 2 * H])
        Vx = sb("Vx", [P, 2, BLK, HP, PW])
        Pr = sb("Pr", [P, 2, 3, 512])
        PTs = sb("PTs", [P, 3, 4, P])
        mx = sb("mx", [P, 3, 8])
        rs = sb("rs", [P, 2, HP + LP, 2])
        grs = sb("grs", [P, 2, H])
        loc = sb("loc", [P, 2, D])
        rem = sb("rem", [P, 2, LD])
        remT = sb("remT", [LD, P])
        att0 = sb("att0", [P, D])
        att = sb("att", [P, D])
        attT = sb("attT", [P, P])
        y = sb("y", [P, 2, D])
        st = sb("st", [P, 2, 6])
        mv = sb("mv", [P, 2, 2])
        rstd = sb("rstd", [P, 2, 1])
        x1 = sb("x1", [P, T, XW])

        before = sb("before", [P, P], BF16)
        ones = sb("ones", [P, P], BF16)
        eint = sb("eint", [P, 2 * E], I32)
        efl = sb("efl", [P, 2 * E])
        tsum = sb("tsum", [P, KT_])
        near = sb("near", [P, KT_])
        off = sb("off", [P, KT_])
        over = sb("over", [P, KT_])
        frac = sb("frac", [P, KT_])
        onehot = sb("onehot", [P, KT_, E], BF16)
        ranks = sb("ranks", [P, KT_ + 1, E])
        nextrow = sb("nextrow", [P, E])
        cand = sb("cand", [P, KT_, E])
        posf = sb("posf", [P, KT_])
        pos = sb("pos", [P, T], U32)
        padrows = sb("padrows", [P, XW])
        tiles = sb("tiles", [1, 4, E + 1])
        table = sb("table", [1, 2 * E + 1], I32)

        w1_s = sb("w1_s", [P, E, F])
        w2_s = sb("w2_s", [P, E, FC, D])
        b1r = sb("b1r", [E * FC, P])
        b1c = sb("b1c", [P, E * FC])
        b2r = sb("b2r", [P, E, D])
        b2s = sb("b2s", [P, E, D])
        xs = sb("xs", [P, XW])
        xk = sb("xk", [P, 2 * XW])
        xsT = sb("xsT", [P, P])
        ha = sb("ha", [P, FC, P])
        hb = sb("hb", [P, FC, P])
        ysum = sb("ysum", [P, D])
        y2 = sb("y2", [P, D])
        st2 = sb("st2", [P, 6])
        mv2 = sb("mv2", [P, 2])
        rstd2 = sb("rstd2", [P, 1])
        yo = sb("yo", [P, D])
        idx = sb("idx", [P, 1], U32)


        bS = [bank(f"bS{j}") for j in range(3)]
        bT = [bank(f"bT{j}") for j in range(2)]
        bV = bank("bV")
        bJ = bank("bJ")
        bL = bank("bL")
        rT, rM, aT, wO = (bL[:, i * P:(i + 1) * P] for i in range(4))

        bA, bB, bX, bY = bS[0], bS[1], bS[2], bV

        x_in = [sem(f"x_in{b}") for b in range(NB)]
        w_in = sem("w_in")
        const_ok = sem("const_ok")
        vconst_ok = sem("vconst_ok")
        pj_ready = sem("pj_ready")
        pj_free = sem("pj_free")
        kx_done = sem("kx_done")
        qg_done = sem("qg_done")
        gk_done = sem("gk_done")
        xp_done = sem("xp_done")
        gat_done = sem("gat_done")
        scores = sem("scores")
        shifted = sem("shifted")
        exped = sem("exped")
        turned = sem("turned")
        turned_out = sem("turned_out")
        pv_done = sem("pv_done")
        normed = sem("normed")
        remT_up = sem("remT_up")
        remT_out = sem("remT_out")
        rem_up = sem("rem_up")
        gated = sem("gated")
        attT_up = sem("attT_up")
        attT_out = sem("attT_out")
        proj_up = sem("proj_up")
        summed = sem("summed")
        stats = sem("stats")
        ln_done = sem("ln_done")
        dve_step = sem("dve_step")
        pool_step = sem("pool_step")
        stored = sem("stored")
        marked = sem("marked")
        placed = sem("placed")
        scattered = sem("scattered")
        padded = sem("padded")
        table_ok = sem("table_ok")
        f_in = sem("f_in")
        b_in = sem("b_in")
        b2_in = sem("b2_in")
        b2_ok = sem("b2_ok")
        tile_in = sem("tile_in")
        kept = sem("kept")
        xT_up = sem("xT_up")
        xT_out = sem("xT_out")
        up_a = sem("up_a")
        up_b = sem("up_b")
        relu_a = sem("relu_a")
        relu_b = sem("relu_b")
        down = sem("down")
        biased = sem("biased")
        y_ok = sem("y_ok")
        bn1 = sem("bn1")
        bn2 = sem("bn2")
        yo_ok = sem("yo_ok")
        out_in = sem("out_in")
        rs1 = sem("rs1")
        rs2 = sem("rs2")
        idx_ok = sem("idx_ok")
        N_W = 10

        def uses_in_slot(t):
            b, k = divmod(t, KT_)
            u = [("V", t)] if t < T else []
            if k == 3 and b >= 1:
                u += [("R", b - 1)]
            if b + 1 < NB:
                u += {0: [("xT", b + 1), ("K", b + 1)], 1: [("Q", b + 1), ("GQ", b + 1)], 2: [("G", b + 1)], 3: []}[k]
            return u

        first_uses = [(n, 0) for n in ("xT", "K", "Q", "GQ", "G", "B")]
        pj = {}
        for use in first_uses + [u for t in range(T) for u in uses_in_slot(t)] + [("R", NB - 1)]:
            pj[use] = len(pj)

        block = ctx.enter_context(nc.Block())

        def load_table(eng, entries, most):
            return [eng.value_load(table[0:1, i:i + 1], min_val=0, max_val=most) for i in entries]

        def ahead(eng, *sems):
            for s in sems:
                eng.sem_inc(s, 1)

        @block.sync
        def _(sp):
            xr = x.rearrange("b (k p) d -> b p k d", p=P)
            for b in range(NB):
                sp.dma_start(x_tok[:, b * KT_:(b + 1) * KT_, :], xr[b]).then_inc(x_in[b], 16)
            sp.dma_start(w1_s[:], W1.rearrange("e p f -> p e f")).then_inc(f_in, 16)
            sp.dma_start(w2_s[:], W2.rearrange("e (c p) d -> p e c d", p=P)).then_inc(f_in, 16)

            sp.wait_ge(table_ok, 1)
            first = load_table(sp, range(E + 1), T + E)
            tail = load_table(sp, range(E + 1, 2 * E + 1), E * SEG - P)
            for e in range(E):
                sp.dma_start(seg[bass.ds(tail[e], P), :], padrows[:]).then_inc(padded, 16)
            sp.wait_ge(padded, 16 * E)
            sp.wait_ge(scattered, 16 * T)

            def load(row):
                sp.dma_start(xs[:], seg[bass.ds(row, P), :]).then_inc(tile_in, 16)

            for e in range(E):
                with sp.Fori(first[e], first[e + 1]) as k:
                    sp.wait_ge(xT_up, k + 1)
                    sp.wait_ge(kept, k + 1)
                    i = nc.s_assert_within(k - first[e], 0, T - 1,
                                           skip_runtime_bounds_check_because="a group has at most all T tiles")
                    load(i * P + e * SEG)
            sp.wait_ge(xT_up, first[E] + 1)
            sp.wait_ge(kept, first[E] + 1)
            load((E - 1) * SEG)

        @block.gpsimd
        def _(pool):
            count = [0]

            def link(ins):
                count[0] += 1
                ins.then_inc(pool_step, 1)
                pool.wait_ge(pool_step, count[0])

            link(nc.gpsimd.memset(ident[:], 0.0))
            link(nc.gpsimd.memset(half[:, 0:1], -0.5))
            link(nc.gpsimd.memset(half[:, 1:2], EPS))
            link(nc.gpsimd.memset(blk16[:], 1.0))
            link(nc.gpsimd.memset(group4[:], 1.0))
            link(nc.gpsimd.memset(sel_l[:], 0.0))
            link(nc.gpsimd.memset(ones[:], 1.0))
            link(nc.gpsimd.memset(before[:], 1.0))
            link(nc.gpsimd.memset(padrows[:], 0.0))
            link(nc.gpsimd.iota(padrows[:, D:XW].bitcast(I32), pattern=[[0, 1]], base=T * P, channel_multiplier=0))
            link(nc.gpsimd.iota(eint[:, 0:E], pattern=[[SEG, E]], base=0, channel_multiplier=0))
            link(nc.gpsimd.iota(eint[:, E:], pattern=[[1, E]], base=-3 * E, channel_multiplier=0))
            link(nc.gpsimd.tensor_copy(efl[:], eint[:]))
            link(nc.gpsimd.tensor_copy(nextrow[:], efl[:, 0:E]))
            link(nc.gpsimd.memset(neg_l[0:W, :], 0.0))
            link(nc.gpsimd.memset(neg_l[W:2 * W, 0:W], NEG))
            link(nc.gpsimd.memset(neg_l[W:2 * W, W:], 0.0))
            link(nc.gpsimd.memset(sel_r[:], 1.0))
            link(nc.gpsimd.memset(neg_r[:], 0.0))

            def keep(v, base, pattern, mult, fill=0.0):
                link(nc.gpsimd.affine_select(out=v, in_=v, compare_op=ALU.is_ge, fill=fill, base=base,
                                             pattern=pattern, channel_multiplier=mult))

            link(nc.gpsimd.affine_select(out=ident[:], in_=ident[:], compare_op=ALU.not_equal, fill=1.0, base=0,
                                         pattern=[[-1, P]], channel_multiplier=1))
            keep(blk16[:], 0, [[-HD, H]], 1)
            keep(blk16[:], HD - 1, [[HD, H]], -1)
            keep(group4[:], 0, [[-W, 4]], 1)
            keep(group4[:], W - 1, [[W, 4]], -1)
            v = sel_l[0:W, :].rearrange("r (n q) -> r n q", q=W)
            link(nc.gpsimd.affine_select(out=v, in_=v, compare_op=ALU.not_equal, fill=1.0, base=0,
                                         pattern=[[0, BLK], [-1, W]], channel_multiplier=1))
            v = sel_l[W:2 * W, 0:W]
            link(nc.gpsimd.affine_select(out=v, in_=v, compare_op=ALU.not_equal, fill=1.0, base=0,
                                         pattern=[[-1, W]], channel_multiplier=1))
            keep(neg_l[0:W, :], -1, [[1, 2 * W]], -1, NEG)
            keep(neg_l[0:W, :], W, [[-1, 2 * W]], 1, NEG)
            keep(sel_r[:], 0, [[1, P]], -CH)
            keep(sel_r[:], CH - 1, [[-1, P]], CH)
            keep(neg_r[:], 0, [[P // CH, KT_], [-1, NL]], 1, NEG)
            keep(before[:], -1, [[1, P]], -1)
            link(nc.gpsimd.memset(wv_par[:], 0.0))
            link(nc.gpsimd.memset(wgv_par[:], 0.0))
            pool.wait_ge(w_in, 16 * N_W)
            for q in range(2):
                for dst, src, n in ((wv_par, wv_s, HP), (wgv_par, wgv_s, LP)):
                    dv = dst[:, q, :].rearrange("p (a c d) -> p a c d", c=2, d=HD)[:, :, q, :]
                    sv = src[:].rearrange("p (a c d) -> p a c d", c=2, d=HD)[:, :, q, :]
                    link(nc.gpsimd.tensor_copy(dv, sv))
            for q in range(2):
                link(nc.gpsimd.tensor_scalar(gmat[:, q * H:(q + 1) * H], blk16[:], gcol[:, q:q + 1], None, ALU.mult))
            link(nc.gpsimd.tensor_tensor(slot4[:], blk16[:, 0:4], blk16[:, 4:8], ALU.add))
            link(nc.gpsimd.tensor_tensor(slot4[:], slot4[:], blk16[:, 8:12], ALU.add))
            link(nc.gpsimd.tensor_tensor(slot4[:], slot4[:], blk16[:, 12:16], ALU.add))
            nc.gpsimd.iota(x1[:, :, D].bitcast(I32), pattern=[[P, T]], base=0, channel_multiplier=1).then_inc(const_ok, 1)

            def expand(dst, src, mask, n):
                return nc.gpsimd.tensor_tensor(
                    dst, src.unsqueeze(1).to_broadcast([src.shape[0], n, src.shape[1]]),
                    mask.unsqueeze(2).to_broadcast([src.shape[0], n, src.shape[1]]), ALU.mult)

            def expand_k(b):
                pool.wait_ge(pj_free, pj[("K", b)] + 1)
                expand(Kx[:, b % 2, :, W:], KT[:, b % 2, :], slot4[:], 4).then_inc(kx_done, 1)

            def expand_q(b):
                pool.wait_ge(pj_free, pj[("Q", b)] + 1)
                expand(Qg[:, b % 2, :, :], QT[:, b % 2, :], group4[:], 4).then_inc(qg_done, 1)

            def expand_gk(b):
                pool.wait_ge(pj_free, pj[("G", b)] + 1)
                expand(GKx[:, b % 2, :, :], GKs[:, b % 2, :], blk16[0:LD, 0:LH], LH).then_inc(gk_done, 1)

            def layernorm(t):
                q = t % 2
                pool.wait_ge(stats, t + 1)
                link(nc.gpsimd.tensor_scalar(rstd[:, q, :], mv[:, q, 1:2], EPS, None, ALU.add))
                link(nc.gpsimd.tensor_tensor(rstd[:, q, :], rstd[:, q, :], half[:, 0:1], ALU.pow))
                nc.gpsimd.tensor_scalar(x1[:, t, 0:D], y[:, q, :], mv[:, q, 0:1], rstd[:, q, :],
                                        ALU.subtract, ALU.mult).then_inc(ln_done, 1)

            def scatter(b):
                pool.wait_ge(placed, b + 1)
                for t in range(b * KT_, (b + 1) * KT_):
                    pool.wait_ge(ln_done, t + 1)
                    nc.gpsimd.indirect_dma_start(seg, bass.IndirectOffsetOnAxis(ap=pos[:, t:t + 1], axis=0),
                                                 x1[:, t, :], None).then_inc(scattered, 16)

            pool.wait_ge(vconst_ok, 1)
            expand_k(0)
            expand_q(0)
            expand_gk(0)
            for t in range(T + 2):
                b, k = divmod(t, KT_)
                if t >= 2:
                    layernorm(t - 2)
                if b + 1 < NB and k < 3:
                    (expand_k, expand_q, expand_gk)[k](b + 1)
                if t == 1:
                    pool.wait_ge(b2_in, 16)
                    nc.gpsimd.tensor_tensor(b2s[:, 0:E - 1, :], b2r[:, 0:E - 1, :], b2r[:, 1:E, :],
                                            ALU.add).then_inc(b2_ok, 1)
                    nc.gpsimd.tensor_tensor(b2s[:, E - 1, :], b2r[:, E - 1, :], b2r[:, 0, :], ALU.add).then_inc(b2_ok, 1)
                if b >= 1 and k == 3:
                    scatter(b - 1)
            scatter(NB - 1)

            pool.wait_ge(table_ok, 1)
            first = load_table(pool, range(E + 1), T + E)

            def keep_rows(k):
                pool.wait_ge(tile_in, (k + 1) * 16)
                nc.gpsimd.tensor_copy(xk[:, bass.ds((k % 2) * XW, XW)], xs[:]).then_inc(kept, 1)

            ahead(pool, kept, yo_ok)

            def store(rows):
                nc.gpsimd.indirect_dma_start(
                    out.rearrange("b s d -> (b s) d"), bass.IndirectOffsetOnAxis(ap=idx[:], axis=0), rows, None,
                    bounds_check=T * P - 1, oob_is_err=False).then_inc(out_in, 16)

            link(nc.gpsimd.tensor_copy(idx[:], padrows[:, D:XW].bitcast(U32)))
            store(padrows[:, 0:D])
            keep_rows(0)
            for e in range(E):
                with pool.Fori(first[e], first[e + 1]) as k:
                    pool.wait_ge(y_ok, k + 1)
                    keep_rows(k + 1)
                    pool.wait_ge(bn2, k + 1)
                    nc.gpsimd.tensor_tensor(rstd2[:], mv2[:, 1:2], half[:, 1:2], ALU.add).then_inc(rs1, 1)
                    pool.wait_ge(rs1, k + 1)
                    nc.gpsimd.tensor_tensor(rstd2[:], rstd2[:], half[:, 0:1], ALU.pow).then_inc(rs2, 1)
                    pool.wait_ge(rs2, k + 1)
                    pool.wait_ge(out_in, k * 16 + 16)
                    nc.gpsimd.tensor_copy(idx[:], xk[:, bass.ds((k % 2) * XW + D, 1)].bitcast(U32)).then_inc(idx_ok, 1)
                    nc.gpsimd.tensor_scalar(yo[:], y2[:], mv2[:, 0:1], rstd2[:, 0:1],
                                            ALU.subtract, ALU.mult).then_inc(yo_ok, 1)
                    pool.wait_ge(table_ok, 1)
                    pool.wait_ge(idx_ok, k + 1)
                    pool.wait_ge(yo_ok, k + 2)
                    store(yo[:])
            pool.wait_ge(table_ok, 1)
            pool.wait_ge(out_in, first[E] * 16 + 16)

        @block.scalar
        def _(act):
            for dst, src in ((wk_s[:], wk), (wq_s[:], wq), (wgq_s[:], wgq), (wgk_s[:], wgk), (wgv_s[:], wgv),
                             (wv_s[:], wv), (gcol[:, 0:1], gate_l.rearrange("h (d a) -> (h d) a", a=1)),
                             (gcol[:, 1:2], gate_r.rearrange("h (d a) -> (h d) a", a=1)),
                             (rout_s[:], r_out_w), (wout_s[:], w_out)):
                act.dma_start(dst, src).then_inc(w_in, 16)
            act.dma_start(b1r[:], b1.rearrange("e (c p) -> (e c) p", p=P)).then_inc(b_in, 16)
            act.dma_start(b2r[:].rearrange("p e d -> p (e d)"),
                          b2.rearrange("e d -> (e d)").partition_broadcast(P)).then_inc(b2_in, 16)

            def take(use):
                kind, n = use
                act.wait_ge(pj_ready, pj[use] + 1)
                q = n % 2
                if kind == "xT":
                    i = nc.scalar.copy(xT[:, q, W:], bJ[:])
                elif kind == "K":
                    i = nc.scalar.copy(KT[:, q, :], bJ[:])
                elif kind == "Q":
                    i = nc.scalar.copy(QT[:, q, :], bJ[:])
                elif kind == "GQ":
                    i = nc.scalar.copy(GQT[:, q, :], bJ[0:LD, :])
                elif kind == "B":
                    i = nc.scalar.copy(b1c[:], bJ[:, 0:E * FC])
                elif kind == "R":
                    if n >= 1:
                        act.wait_ge(placed, n)
                    i = nc.scalar.copy(ranks[:].rearrange("p k e -> p (k e)"), bJ[:, 0:(KT_ + 1) * E])
                elif kind == "V":
                    if n >= 2:
                        act.wait_ge(pv_done, 3 * (n - 1))
                    i = nc.scalar.copy(Vx[:, q, :, :, 0:2 * HD],
                                       bJ[:].rearrange("p (n a c) -> p n a c", n=BLK, c=2 * HD))
                else:
                    nc.scalar.mul(GKs[:, q, :], bJ[0:LD, 0:NL], 1.0 / CH)
                    nc.scalar.mul(GVx[:, q, :, 0:2 * HD],
                                  bJ[:, NL:NL + LD].rearrange("p (a c) -> p a c", c=2 * HD), 1.0 / CH)
                    i = nc.scalar.activation(gex[:, q, :, :],
                                             bJ[:, P:P + KT_ * 2 * H].rearrange("p (k g) -> p k g", k=KT_),
                                             ACT.Exp, scale=-1.0)
                i.then_inc(pj_free, 1)

            def exp(t, j):
                act.wait_ge(shifted, 3 * t + j + 1)
                v = Pr[:, t % 2, j, :]
                nc.scalar.activation(v, v, ACT.Exp, scale=SCALE).then_inc(exped, 1)

            def turned_copy(t, j):
                u = 3 * t + j
                act.wait_ge(turned, u + 1)
                if t >= 1:
                    act.wait_ge(pv_done, u - 2)
                nc.scalar.copy(PTs[:, j, :, :], bT[u % 2][:].rearrange("p (c q) -> p c q", c=4)).then_inc(turned_out, 1)

            act.wait_ge(vconst_ok, 1)
            for use in first_uses:
                take(use)
            for t in range(T + 2):
                uses = uses_in_slot(t)
                for j in range(3):
                    if j < len(uses):
                        take(uses[j])
                    if 1 <= t <= T:
                        turned_copy(t - 1, j)
                    if t < T:
                        exp(t, j)
                    if t >= 2 and j == 0:
                        act.wait_ge(remT_up, t - 1)
                        nc.scalar.copy(remT[:], rT[0:LD, :]).then_inc(remT_out, 1)
                    if t >= 2 and j == 2:
                        act.wait_ge(attT_up, t - 1)
                        nc.scalar.copy(attT[:], aT).then_inc(attT_out, 1)
            take(("R", NB - 1))

            act.wait_ge(table_ok, 1)
            first = load_table(act, range(E + 1), T + E)
            ahead(act, relu_a)
            for e in range(E):
                with act.Fori(first[e], first[e + 1]) as k:
                    act.wait_ge(up_a, k + 1)
                    act.wait_ge(down, k + 1)
                    for c in range(FC):
                        nc.scalar.activation(ha[:, c, :], bA[:, c * P:(c + 1) * P], ACT.Relu,
                                             bias=b1c[:, e * FC + c:e * FC + c + 1]).then_inc(relu_a, 1)

        @block.vector
        def _(dve):
            count = [0]

            def link(ins):
                count[0] += 1
                ins.then_inc(dve_step, 1)
                dve.wait_ge(dve_step, count[0])

            nc.vector.memset(xT[:, :, 0:W], 0.0)
            nc.vector.memset(Kx[:, :, :, 0:W], 0.0)
            nc.vector.memset(Vx[0:64, :, :, :, 2 * HD:2 * HD + 1], 1.0)
            nc.vector.memset(Vx[64:P, :, :, :, 2 * HD:2 * HD + 1], 0.0)
            nc.vector.memset(Vx[0:64, :, :, :, 2 * HD + 1:], 0.0)
            nc.vector.memset(Vx[64:P, :, :, :, 2 * HD + 1:], 1.0)
            nc.vector.memset(GVx[0:64, :, :, 2 * HD:2 * HD + 1], 1.0)
            nc.vector.memset(GVx[64:P, :, :, 2 * HD:2 * HD + 1], 0.0)
            nc.vector.memset(GVx[0:64, :, :, 2 * HD + 1:], 0.0)
            nc.vector.memset(GVx[64:P, :, :, 2 * HD + 1:], 1.0).then_inc(vconst_ok, 1)

            def pooled(b):
                dve.wait_ge(pj_free, pj[("xT", b)] + 1)
                nc.vector.tensor_reduce(xp[:, b % 2, :], xT[:, b % 2, W:].rearrange("p (n c) -> p n c", c=CH),
                                        AX.X, ALU.add).then_inc(xp_done, 1)

            def gates(b):
                dve.wait_ge(pj_free, pj[("G", b)] + 1)
                g = gat[:, b % 2, :, :]
                link(nc.vector.tensor_scalar(g, gex[:, b % 2, :, :], 1.0, None, ALU.add))
                link(nc.vector.reciprocal(g, g))

            def shift(t, j):
                u = 3 * t + j
                dve.wait_ge(scores, u + 1)
                s = bS[j][:].rearrange("p (h k) -> p h k", h=8)
                link(nc.vector.tensor_reduce(mx[:, j, :], s, AX.X, ALU.max))
                if t >= 2:
                    dve.wait_ge(turned, u - 5)
                nc.vector.tensor_tensor(Pr[:, t % 2, j, :].rearrange("p (h k) -> p h k", h=8), s,
                                        mx[:, j, :].unsqueeze(2).to_broadcast([P, 8, 2 * W]),
                                        ALU.subtract).then_inc(shifted, 1)

            def normalise(t):
                q, b, k = t % 2, t // KT_, t % KT_
                dve.wait_ge(pv_done, 3 * t + 3)
                pv = bV[:, 0:(HP + LP) * PW].rearrange("p (a c) -> p a c", c=PW)
                link(nc.vector.reciprocal(rs[:, q, :, :], pv[:, :, 2 * HD:]))
                link(nc.vector.tensor_tensor(grs[:, q, :], rs[:, q, 0:HP, :].rearrange("p a c -> p (a c)"),
                                             gat[:, b % 2, k, 0:H], ALU.mult))
                nc.vector.tensor_tensor(
                    loc[:, q, :].rearrange("p (a c d) -> p a c d", c=2, d=HD),
                    pv[:, 0:HP, 0:2 * HD].rearrange("p a (c d) -> p a c d", c=2),
                    grs[:, q, :].rearrange("p (a c) -> p a c", c=2).unsqueeze(3).to_broadcast([P, HP, 2, HD]), ALU.mult)
                nc.vector.tensor_tensor(
                    rem[:, q, :].rearrange("p (a c d) -> p a c d", c=2, d=HD),
                    pv[:, HP:, 0:2 * HD].rearrange("p a (c d) -> p a c d", c=2),
                    rs[:, q, HP:, :].unsqueeze(3).to_broadcast([P, LP, 2, HD]), ALU.mult).then_inc(normed, 1)

            def gate(t):
                q, b, k = t % 2, t // KT_, t % KT_
                dve.wait_ge(rem_up, t + 1)
                if t >= 1:
                    dve.wait_ge(attT_up, t)
                link(nc.vector.tensor_tensor(
                    att0[:].rearrange("p (h d) -> p h d", d=HD), rM.rearrange("p (h d) -> p h d", d=HD),
                    gat[:, b % 2, k, H:].unsqueeze(2).to_broadcast([P, H, HD]), ALU.mult))
                nc.vector.tensor_tensor(att[:], att0[:], loc[:, q, :], ALU.add).then_inc(gated, 1)

            def residual(t):
                q = t % 2
                dve.wait_ge(proj_up, t + 1)
                if t >= 2:
                    dve.wait_ge(ln_done, t - 1)
                ins = nc.vector.tensor_tensor(y[:, q, :], wO, x_tok[:, t, :], ALU.add)
                ins.then_inc(summed, 1)
                dve.wait_ge(summed, t + 1)
                link(nc.vector.bn_stats(st[:, q, :], y[:, q, :]))
                nc.vector.bn_aggr(mv[:, q, :], st[:, q, :]).then_inc(stats, 1)

            def mark(b):
                dve.wait_ge(ln_done, (b + 1) * KT_)
                v = x1[:, b * KT_:(b + 1) * KT_, :]
                link(nc.vector.tensor_tensor(tsum[:], v[:, :, 0], v[:, :, 1], ALU.add))
                link(nc.vector.tensor_scalar(near[:], tsum[:], ROUND, -ROUND, ALU.add, ALU.add))
                link(nc.vector.tensor_tensor(off[:], near[:], tsum[:], ALU.subtract))
                nc.vector.tensor_scalar(over[:], off[:], 0.0, None, ALU.is_gt)
                link(nc.vector.tensor_scalar(frac[:], off[:], 0.0, None, ALU.not_equal))
                link(nc.vector.tensor_tensor(near[:], near[:], over[:], ALU.subtract))
                link(nc.vector.scalar_tensor_tensor(frac[:], tsum[:], 0.0, frac[:], ALU.is_lt, ALU.mult))
                link(nc.vector.tensor_tensor(near[:], near[:], frac[:], ALU.add))
                link(nc.vector.tensor_scalar(off[:], near[:], 1.0 / E, 3.0 - 0.5 + 0.5 / E, ALU.mult, ALU.add))
                link(nc.vector.tensor_scalar(off[:], off[:], ROUND, -ROUND, ALU.add, ALU.add))
                link(nc.vector.scalar_tensor_tensor(near[:], off[:], -float(E), near[:], ALU.mult, ALU.add))
                nc.vector.tensor_tensor(onehot[:], near[:].unsqueeze(2).to_broadcast([P, KT_, E]),
                                        efl[:, E:].unsqueeze(1).to_broadcast([P, KT_, E]),
                                        ALU.is_equal).then_inc(marked, 1)

            def place(b):
                dve.wait_ge(marked, b + 1)
                dve.wait_ge(pj_free, pj[("R", b)] + 1)
                link(nc.vector.tensor_tensor(cand[:], ranks[:, 0:KT_, :],
                                             nextrow[:].unsqueeze(1).to_broadcast([P, KT_, E]), ALU.add))
                link(nc.vector.tensor_tensor(cand[:], cand[:], onehot[:], ALU.mult))
                link(nc.vector.tensor_reduce(posf[:], cand[:], AX.X, ALU.add))
                link(nc.vector.tensor_tensor(nextrow[:], nextrow[:], ranks[:, KT_, :], ALU.add))
                nc.vector.tensor_copy(pos[:, b * KT_:(b + 1) * KT_], posf[:]).then_inc(placed, 1)

            def count_tiles():
                n, m = tiles[:, 0, :], tiles[:, 1, :]
                link(nc.vector.memset(tiles[:], 0.0))
                link(nc.vector.tensor_tensor(m[:, 1:], nextrow[0:1, :], efl[0:1, 0:E], ALU.subtract))
                link(nc.vector.tensor_scalar(m[:, 1:], m[:, 1:], 1.0 / P, 0.5 - 0.5 / P, ALU.mult, ALU.add))
                link(nc.vector.tensor_scalar(m[:, 1:], m[:, 1:], ROUND, -ROUND, ALU.add, ALU.add))
                link(nc.vector.tensor_scalar(n[:, 1:], m[:, 1:], 1.0, None, ALU.max))
                src, dst, d = n, m, 1
                while d <= E:
                    link(nc.vector.tensor_copy(dst[:, 0:d], src[:, 0:d]))
                    link(nc.vector.tensor_tensor(dst[:, d:], src[:, d:], src[:, 0:E + 1 - d], ALU.add))
                    src, dst, d = dst, (tiles[:, 2, :] if dst is m else m), 2 * d
                link(nc.vector.tensor_copy(table[:, 0:E + 1], src))
                nc.vector.tensor_copy(table[:, E + 1:], nextrow[0:1, :]).then_inc(table_ok, 1)

            pooled(0)
            gates(0)
            for t in range(T + 2):
                b, k = divmod(t, KT_)
                if t >= 2:
                    normalise(t - 2)
                if t < T:
                    shift(t, 0)
                    if k == 1 and b + 1 < NB:
                        pooled(b + 1)
                    shift(t, 1)
                    if k == 3 and b + 1 < NB:
                        gates(b + 1)
                if t >= 2:
                    gate(t - 2)
                if t < T:
                    shift(t, 2)
                if t >= 2:
                    residual(t - 2)
                if b >= 1 and k == 2 and t < T:
                    mark(b - 1)
                if b >= 1 and k == 3:
                    place(b - 1)
            mark(NB - 1)
            place(NB - 1)
            count_tiles()

            dve.wait_ge(table_ok, 1)
            dve.wait_ge(b2_ok, 2)
            first = load_table(dve, range(E + 1), T + E)

            def column_copy(k):
                dve.wait_ge(xT_up, k + 2)
                dve.wait_ge(up_b, k + 1)
                nc.vector.tensor_copy(xsT[:], bX[:, 0:P]).then_inc(xT_out, 1)

            ahead(dve, xT_out, relu_b, biased, y_ok)
            column_copy(0)
            for e in range(E):
                a = (e + 1) % E
                with dve.Fori(first[e], first[e + 1]) as k:
                    dve.wait_ge(up_b, k + 2)
                    dve.wait_ge(down, k + 1)
                    for c in range(FC):
                        nc.vector.tensor_scalar(hb[:, c, :], bB[:, c * P:(c + 1) * P], b1c[:, a * FC + c:a * FC + c + 1],
                                                0.0, ALU.add, ALU.max).then_inc(relu_b, 1)
                    column_copy(k + 1)
                    dve.wait_ge(down, k + 2)
                    nc.vector.tensor_tensor(ysum[:], bY[:, 0:D], b2s[:, e, :], ALU.add).then_inc(biased, 1)
                    dve.wait_ge(biased, k + 2)
                    dve.wait_ge(kept, k + 2)
                    dve.wait_ge(yo_ok, k + 1)
                    nc.vector.scalar_tensor_tensor(y2[:], ysum[:], 0.5, xk[:, bass.ds((k % 2) * XW, D)],
                                                   ALU.mult, ALU.add).then_inc(y_ok, 1)
                    dve.wait_ge(y_ok, k + 2)
                    nc.vector.bn_stats(st2[:], y2[:]).then_inc(bn1, 1)
                    dve.wait_ge(table_ok, 1)
                    dve.wait_ge(bn1, k + 1)
                    nc.vector.bn_aggr(mv2[:], st2[:]).then_inc(bn2, 1)

        @block.tensor
        def _(pe):
            mm = nc.tensor.matmul

            def fill(use):
                kind, n = use
                if pj[use] >= 1:
                    pe.wait_ge(pj_free, pj[use])
                q = n % 2
                if kind == "xT":
                    pe.wait_ge(x_in[n], 16)
                    for i in range(KT_):
                        last = nc.tensor.transpose(bJ[:, i * P:(i + 1) * P], x_tok[:, n * KT_ + i, :], ident[:])
                elif kind == "K":
                    last = mm(bJ[:], wk_s[:], xT[:, q, W:], start=True, stop=True)
                elif kind == "Q":
                    last = mm(bJ[:], wq_s[:], xT[:, q, W:], start=True, stop=True)
                elif kind == "GQ":
                    last = mm(bJ[0:LD, :], wgq_s[:], xT[:, q, W:], start=True, stop=True)
                elif kind == "B":
                    pe.wait_ge(b_in, 16)
                    last = nc.tensor.transpose(bJ[:, 0:E * FC], b1r[:], ident[0:E * FC, 0:E * FC])
                elif kind == "R":
                    pe.wait_ge(marked, n + 1)
                    oh = onehot[:].rearrange("p k e -> p (k e)")
                    mm(bJ[:, 0:KT_ * E], before[:], oh, start=True, stop=False, skip_group_check=True)
                    for i in range(1, KT_ + 1):
                        last = mm(bJ[:, i * E:(KT_ + 1) * E], ones[:], oh[:, 0:(KT_ + 1 - i) * E], start=False,
                                  stop=(i == KT_), skip_group_check=True)
                elif kind == "G":
                    pe.wait_ge(xp_done, n + 1)
                    mm(bJ[0:LD, 0:NL], wgk_s[:], xp[:, q, :], start=True, stop=True)
                    for c in range(2):
                        mm(bJ[64 * c:64 * c + 64, NL:NL + LD], xp[:, q, :], wgv_par[:, c, :], start=True, stop=True)
                    for i in range(KT_):
                        last = mm(bJ[:, P + i * 2 * H:P + (i + 1) * 2 * H], QT[:, q, i * P:(i + 1) * P], gmat[:],
                                  start=True, stop=True)
                else:
                    b, k = divmod(n, KT_)
                    for i in range(BLK):
                        o = k * P + i * W
                        for c in range(2):
                            last = mm(bJ[64 * c:64 * c + 64, i * P:(i + 1) * P], xT[:, b % 2, o:o + 2 * W],
                                      wv_par[:, c, :], start=True, stop=True)
                last.then_inc(pj_ready, 1)

            def score(t, j):
                u, b, k = 3 * t + j, t // KT_, t % KT_
                q = b % 2
                if t >= 1:
                    pe.wait_ge(shifted, u - 2)
                if j < 2:
                    rows = 2 * W if k == 0 else W
                    mm(bS[j][:], sel_l[0:rows, :], neg_l[0:rows, :].unsqueeze(1).to_broadcast([rows, 8, 2 * W]),
                       start=True, stop=False, skip_group_check=True)
                    if k == 0 and j == 0:
                        pe.wait_ge(kx_done, b + 1)
                        pe.wait_ge(qg_done, b + 1)
                    for g in range(2):
                        for i in range(BLK):
                            o = k * P + i * W
                            last = mm(bS[j][i * W:(i + 1) * W, g * 256:(g + 1) * 256],
                                      Qg[:, q, 2 * j + g, o:o + W], Kx[:, q, :, o:o + 2 * W],
                                      start=False, stop=(g == 1), skip_group_check=True)
                else:
                    if k == 0:
                        pe.wait_ge(gk_done, b + 1)
                    mm(bS[j][:], sel_r[:], neg_r[:, k, :].unsqueeze(1).to_broadcast([P // CH, LH, NL]),
                       start=True, stop=False)
                    last = mm(bS[j][:], GQT[:, q, k * P:(k + 1) * P], GKx[:, q, :, :].rearrange("p h n -> p (h n)"),
                              start=False, stop=True)
                last.then_inc(scores, 1)

            def turn(t, j):
                u = 3 * t + j
                pe.wait_ge(exped, u + 1)
                if u >= 2:
                    pe.wait_ge(turned_out, u - 1)
                for c in range(4):
                    last = nc.tensor.transpose(bT[u % 2][:, c * P:(c + 1) * P], Pr[:, t % 2, j, c * P:(c + 1) * P], ident[:])
                last.then_inc(turned, 1)

            def weigh(t, j):
                u, q = 3 * t + j, t % 2
                pe.wait_ge(turned_out, u + 1)
                if j == 0:
                    pe.wait_ge(pj_free, pj[("V", t)] + 1)
                    if t >= 1:
                        pe.wait_ge(normed, t)
                for c in range(4):
                    a = 4 * j + c
                    if j < 2:
                        for i in range(BLK):
                            last = mm(bV[i * W:(i + 1) * W, a * PW:(a + 1) * PW], PTs[:, j, c, i * W:(i + 1) * W],
                                      Vx[:, q, i, a, :], start=True, stop=True)
                    else:
                        last = mm(bV[:, a * PW:(a + 1) * PW], PTs[:, j, c, :], GVx[:, (t // KT_) % 2, c, :],
                                  start=True, stop=True)
                last.then_inc(pv_done, 1)

            pe.wait_ge(const_ok, 1)
            pe.wait_ge(w_in, 16 * N_W)
            for use in first_uses:
                fill(use)
            for t in range(T + 2):
                uses = uses_in_slot(t)
                for j in range(3):
                    if j < len(uses):
                        fill(uses[j])
                    if t < T:
                        score(t, j)
                    if 1 <= t <= T:
                        turn(t - 1, j)
                        if j >= 1:
                            weigh(t - 1, j - 1)
                    if t >= 2:
                        s = t - 2
                        if j == 0:
                            pe.wait_ge(normed, s + 1)
                            if s >= 1:
                                pe.wait_ge(summed, s)
                            nc.tensor.transpose(rT[0:LD, :], rem[:, s % 2, :], ident[:]).then_inc(remT_up, 1)
                        elif j == 1:
                            pe.wait_ge(remT_out, s + 1)
                            mm(rM, remT[:], rout_s[:], start=True, stop=True).then_inc(rem_up, 1)
                        else:
                            pe.wait_ge(gated, s + 1)
                            nc.tensor.transpose(aT, att[:], ident[:]).then_inc(attT_up, 1)
                if 1 <= t <= T:
                    weigh(t - 1, 2)
                if t >= 2:
                    s = t - 2
                    pe.wait_ge(attT_out, s + 1)
                    mm(wO, attT[:], wout_s[:], start=True, stop=True).then_inc(proj_up, 1)
            fill(("R", NB - 1))

            pe.wait_ge(table_ok, 1)
            pe.wait_ge(f_in, 32)
            first = load_table(pe, range(E + 1), T + E)

            def columns(k):
                pe.wait_ge(tile_in, (k + 1) * 16)
                pe.wait_ge(xT_out, k + 1)
                nc.tensor.transpose(bX[:, 0:P], xs[:, 0:D], ident[:]).then_inc(xT_up, 1)

            ahead(pe, xT_up, up_b, down)
            columns(0)
            for e in range(E):
                a = (e + 1) % E
                with pe.Fori(first[e], first[e + 1]) as k:
                    pe.wait_ge(xT_out, k + 2)
                    pe.wait_ge(relu_a, k * FC + 1)
                    for c in range(FC):
                        last = mm(bA[:, c * P:(c + 1) * P], w1_s[:, e, c * P:(c + 1) * P], xsT[:], start=True, stop=True)
                    last.then_inc(up_a, 1)
                    pe.wait_ge(relu_b, k * FC + 1)
                    for c in range(FC):
                        last = mm(bB[:, c * P:(c + 1) * P], w1_s[:, a, c * P:(c + 1) * P], xsT[:], start=True, stop=True)
                    last.then_inc(up_b, 1)
                    pe.wait_ge(biased, k + 1)
                    for c in range(FC):
                        pe.wait_ge(relu_a, k * FC + c + 2)
                        mm(bY[:, 0:D], ha[:, c, :], w2_s[:, e, c, :], start=(c == 0), stop=False)
                    columns(k + 1)
                    for c in range(FC):
                        pe.wait_ge(relu_b, k * FC + c + 2)
                        last = mm(bY[:, 0:D], hb[:, c, :], w2_s[:, a, c, :], start=False, stop=(c == FC - 1))
                    last.then_inc(down, 1)


_INS = ["L0_attn_x", "L0_attn_wq", "L0_attn_wk", "L0_attn_wv", "L0_attn_wgq", "L0_attn_wgk", "L0_attn_wgv",
        "L0_attn_r_out_w", "L0_attn_gate_local_w", "L0_attn_gate_remote_w", "L0_attn_w_out",
        "L0_ffn_W1", "L0_ffn_b1", "L0_ffn_W2", "L0_ffn_b2"]


def kernel(**inputs):
    import numpy as _np
    import concourse.bacc as _bacc
    from concourse import mybir as _mybir
    from concourse.bass_utils import run_bass_kernel_spmd as _run

    nc = _bacc.Bacc("TRN2", target_bir_lowering=False, num_devices=1)
    arrays, args = {}, []
    for name in _INS:
        a = _np.ascontiguousarray(inputs[name])
        arrays[f"in_{name}"] = a
        args.append(nc.dram_tensor(f"in_{name}", a.shape, _mybir.dt.from_np(a.dtype), kind="ExternalInput").ap())
    shape = inputs["L0_attn_x"].shape
    args.append(nc.dram_tensor("out0", shape, F32, kind="ExternalOutput").ap())
    n = shape[0] * shape[1]
    experts = inputs["L0_ffn_W1"].shape[0]
    args.append(nc.dram_tensor("groups", (experts * (n + P), P + 1), F32, kind="Internal").ap())
    bass_windowed_latent_attention_hash_moe(nc, *args)
    r = _run(nc, [arrays], core_ids=[0])
    return r.results[0]["out0"]
```

```python
from contextlib import ExitStack

import concourse.bass as bass
from concourse import mybir

ALU = mybir.AluOpType
ACT = mybir.ActivationFunctionType
AX = mybir.AxisListType
F32 = mybir.dt.float32
BF16 = mybir.dt.bfloat16
I32 = mybir.dt.int32
U32 = mybir.dt.uint32

P = 128
NEG = -1.0e30
ROUND = 12582912.0


def bass_windowed_latent_attention_hash_moe(
    nc, x, wq, wk, wv, wgq, wgk, wgv, r_out_w, gate_l, gate_r, w_out, W1, b1, W2, b2, out, seg,
):
    NB, S, D = x.shape
    H, HD = gate_l.shape
    LD = wgq.shape[1]
    LH = LD // HD
    W = 32
    NL = 64
    CH = S // NL
    E, _, F = W1.shape
    FC = F // P
    KT_ = S // P
    T = NB * KT_
    BLK = P // W
    HP = H // 2
    LP = LH // 2
    PW = 2 * HD + 2
    SCALE = float(HD) ** -0.5
    EPS = 1e-5
    SEG = seg.shape[0] // E
    RING = 4
    XW = D + 1

    with ExitStack() as ctx:
        def sb(name, shape, dt=F32):
            return ctx.enter_context(nc.sbuf_tensor(name, shape, dt))

        def bank(name, dt=F32):
            return ctx.enter_context(nc.psum_tensor(name, [P, 512], dt))

        def sem(name):
            return ctx.enter_context(nc.semaphore(name))

        x_tok = sb("x_tok", [P, T, D])
        wq_s, wk_s, wv_s, wout_s = (sb(n, [P, P]) for n in ("wq_s", "wk_s", "wv_s", "wout_s"))
        wgq_s, wgk_s = (sb(n, [P, P]) for n in ("wgq_s", "wgk_s"))
        wgv_s = sb("wgv_s", [P, LD])
        rout_s = sb("rout_s", [P, P])
        gcol = sb("gcol", [P, 2])
        ident = sb("ident", [P, P])
        warm = sb("warm", [1, 1])
        half = sb("half", [P, 2])
        blk16 = sb("blk16", [P, H])
        slot4 = sb("slot4", [P, 4])
        group4 = sb("group4", [P, 4])
        gmat = sb("gmat", [P, 2 * H])
        sel_l = sb("sel_l", [P, P], BF16)
        neg_l = sb("neg_l", [P, 2, 2 * W], BF16)
        sel_r = sb("sel_r", [P, P], BF16)
        neg_r = sb("neg_r", [P, KT_, NL], BF16)

        xT = sb("xT", [P, 2, W + S])
        KT = sb("KT", [P, 2, S])
        QT = sb("QT", [P, 2, S])
        Kx = sb("Kx", [P, 2, 4, W + S])
        Qg = sb("Qg", [P, 2, 4, S])
        xp = sb("xp", [P, 2, NL])
        GQT = sb("GQT", [P, 2, S])
        GKs = sb("GKs", [P, 2, NL])
        GKx = sb("GKx", [P, 2, LH, NL])
        GVx = sb("GVx", [P, 2, LP, PW])
        gex = sb("gex", [P, 2, KT_, 2 * H])
        gat = sb("gat", [P, 2, KT_, 2 * H])
        Vx = sb("Vx", [P, 2, BLK, HP, PW])
        Pr = sb("Pr", [P, 2, 3, 512])
        PTs = sb("PTs", [P, 3, 4, P])
        mx = sb("mx", [P, 3, 8])
        rs = sb("rs", [P, 2, HP + LP, 2])
        grs = sb("grs", [P, 2, H])
        loc = sb("loc", [P, 2, D])
        rem = sb("rem", [P, 2, P])
        remT = sb("remT", [P, P])
        att0 = sb("att0", [P, D])
        att = sb("att", [P, D])
        attT = sb("attT", [P, P])
        y = sb("y", [P, 2, D])
        st = sb("st", [P, 2, 6])
        mv = sb("mv", [P, 2, 2])
        rstd = sb("rstd", [P, 2, 1])
        x1 = sb("x1", [P, T, XW])

        before = sb("before", [P, P], BF16)
        ones = sb("ones", [P, P], BF16)
        eint = sb("eint", [P, 2 * E], I32)
        efl = sb("efl", [P, 2 * E])
        tsum = sb("tsum", [P, KT_])
        near = sb("near", [P, KT_])
        off = sb("off", [P, KT_])
        over = sb("over", [P, KT_])
        frac = sb("frac", [P, KT_])
        onehot = sb("onehot", [P, KT_, E], BF16)
        ranks = sb("ranks", [P, KT_ + 1, E])
        nextrow = sb("nextrow", [P, E])
        cand = sb("cand", [P, KT_, E])
        posf = sb("posf", [P, KT_])
        pos = sb("pos", [P, T], U32)
        padrows = sb("padrows", [P, XW])
        tiles = sb("tiles", [1, 4, E + 1])
        tail_table = sb("tail_table", [1, E], I32)
        tile_table = sb("tile_table", [1, E + 1], I32)

        w1_s = sb("w1_s", [P, E, F])
        w2_s = sb("w2_s", [P, E, FC, D])
        b1r = sb("b1r", [E * FC, P])
        b1c = sb("b1c", [P, E * FC])
        b2r = sb("b2r", [P, E, D])
        b2s = sb("b2s", [P, E, D])
        xs = sb("xs", [P, XW])
        xk = sb("xk", [P, RING * XW])
        xsT = sb("xsT", [P, P])
        ha = sb("ha", [P, FC, P])
        hb = sb("hb", [P, FC, P])
        ysum = sb("ysum", [P, D])
        y2 = sb("y2", [P, D])
        st2 = sb("st2", [P, 6])
        mv2 = sb("mv2", [P, 2])
        rstd2 = sb("rstd2", [P, 1])
        yo = sb("yo", [P, D])
        idx = sb("idx", [P, 1], U32)


        bS = [bank(f"bS{j}") for j in range(3)]
        bT = [bank(f"bT{j}") for j in range(2)]
        bV = bank("bV")
        bJ = bank("bJ")
        bL = bank("bL")
        rT, rM, aT, wO = (bL[:, i * P:(i + 1) * P] for i in range(4))

        bA, bB, bX, bY = bS[0], bS[1], bS[2], bV

        x_in = [sem(f"x_in{b}") for b in range(NB)]
        wk_in, wq_in, wgq_in, wg_in, wv_in, wo_in, g_in = (
            sem(n) for n in ("wk_in", "wq_in", "wgq_in", "wg_in", "wv_in", "wo_in", "g_in"))
        gmat_ok = sem("gmat_ok")
        ident_ok = sem("ident_ok")
        heads_ok = sem("heads_ok")
        masks_ok = sem("masks_ok")
        vconst_ok = sem("vconst_ok")
        pj_ready = sem("pj_ready")
        pj_free = sem("pj_free")
        kx_done = sem("kx_done")
        qg_done = sem("qg_done")
        gk_done = sem("gk_done")
        xp_done = sem("xp_done")
        gat_done = sem("gat_done")
        scores = sem("scores")
        shifted = sem("shifted")
        exped = sem("exped")
        turned = sem("turned")
        turned_out = sem("turned_out")
        pv_done = sem("pv_done")
        normed = sem("normed")
        remT_up = sem("remT_up")
        remT_out = sem("remT_out")
        rem_up = sem("rem_up")
        gated = sem("gated")
        attT_up = sem("attT_up")
        attT_out = sem("attT_out")
        proj_up = sem("proj_up")
        summed = sem("summed")
        stats = sem("stats")
        ln_done = sem("ln_done")
        dve_step = sem("dve_step")
        pool_step = sem("pool_step")
        stored = sem("stored")
        marked = sem("marked")
        placed = sem("placed")
        scattered = sem("scattered")
        padded = sem("padded")
        tails_ok = sem("tails_ok")
        table_ok = sem("table_ok")
        f_in = sem("f_in")
        b_in = sem("b_in")
        b2_in = sem("b2_in")
        b2_ok = sem("b2_ok")
        tile_in = sem("tile_in")
        kept = sem("kept")
        xT_up = sem("xT_up")
        xT_out = sem("xT_out")
        up_a = sem("up_a")
        up_b = sem("up_b")
        relu_a = sem("relu_a")
        relu_b = sem("relu_b")
        down = sem("down")
        biased = sem("biased")
        y_ok = sem("y_ok")
        bn1 = sem("bn1")
        bn2 = sem("bn2")
        yo_ok = sem("yo_ok")
        out_in = sem("out_in")
        rs1 = sem("rs1")
        rs2 = sem("rs2")
        idx_ok = sem("idx_ok")

        def others(t):
            b, k = divmod(t, KT_)
            u = []
            if b + 1 < NB:
                u += {0: [("xT", b + 1), ("K", b + 1)], 1: [("Q", b + 1), ("GQ", b + 1)], 2: [("G", b + 1)], 3: []}[k]
            if k == 0 and 2 <= b <= NB:
                u.append(("R", b - 2))
            if t == 2:
                u.append(("B", 0))
            return u

        first_uses = [(n, 0) for n in ("xT", "K", "Q")]
        early_uses = [(n, 0) for n in ("GQ", "G")]
        pj = {}
        for use in (first_uses + [("V", 0)] + early_uses + others(0)
                    + [u for t in range(1, T + 1) for u in [("V", t)] * (t < T) + others(t)] + [("R", NB - 1)]):
            pj[use] = len(pj)
        early_bank = {("K", 0): bT[0], ("Q", 0): bT[1], ("GQ", 0): bV, ("G", 0): bL}

        block = ctx.enter_context(nc.Block())

        def load_table(eng, tab, entries, ready, most):
            eng.wait_ge(ready, 1)
            return [eng.value_load(tab[0:1, i:i + 1], min_val=0, max_val=most) for i in entries]

        def pad_tails(eng, groups):
            tail = load_table(eng, tail_table, groups, tails_ok, E * SEG - P)
            for row in tail:
                eng.dma_start(seg[bass.ds(row, P), :], padrows[:]).then_inc(padded, 16)

        def expand(eng, dst, src, mask, n):
            return eng.tensor_tensor(
                dst, src.unsqueeze(1).to_broadcast([src.shape[0], n, src.shape[1]]),
                mask.unsqueeze(2).to_broadcast([src.shape[0], n, src.shape[1]]), ALU.mult)

        def ahead(eng, *sems, by=1):
            for s in sems:
                eng.sem_inc(s, by)

        @block.sync
        def _(sp):
            xr = x.rearrange("b (k p) d -> b p k d", p=P)
            def load_x(b):
                sp.dma_start(x_tok[:, b * KT_:(b + 1) * KT_, :], xr[b]).then_inc(x_in[b], 16)

            load_x(0)
            for dst, src, s in ((wv_s[:], wv, wv_in), (wgq_s[:, 0:LD], wgq, wgq_in),
                                (gcol[:, 0:1], gate_l.rearrange("h (d a) -> (h d) a", a=1), g_in),
                                (gcol[:, 1:2], gate_r.rearrange("h (d a) -> (h d) a", a=1), g_in),
                                (wgk_s[:, 0:LD], wgk, wg_in), (wgv_s[:], wgv, wg_in),
                                (rout_s[0:LD, :], r_out_w, wo_in), (wout_s[:], w_out, wo_in)):
                sp.dma_start(dst, src).then_inc(s, 16)
            load_x(1)
            sp.dma_start(b1r[:], b1.rearrange("e (c p) -> (e c) p", p=P)).then_inc(b_in, 16)
            for b in range(2, NB):
                load_x(b)
            for b in range(NB):
                sp.wait_ge(x_in[b], 16)
            sp.dma_start(b2r[:].rearrange("p e d -> p (e d)"),
                         b2.rearrange("e d -> (e d)").partition_broadcast(P)).then_inc(b2_in, 16)
            sp.dma_start(w1_s[:], W1.rearrange("e p f -> p e f")).then_inc(f_in, 16)
            sp.dma_start(w2_s[:], W2.rearrange("e (c p) d -> p e c d", p=P)).then_inc(f_in, 16)

            pad_tails(sp, range(0, E, 2))
            first = load_table(sp, tile_table, range(E + 1), table_ok, T + E)
            sp.wait_ge(padded, 16 * E)
            sp.wait_ge(scattered, 16 * T)

            def load(row, k):
                sp.dma_start(xs[:], seg[bass.ds(row, P), :]).then_inc(tile_in, 16)
                sp.dma_start(xk[:, bass.ds((k % RING) * XW, XW)], seg[bass.ds(row, P), :]).then_inc(kept, 16)

            for e in range(E):
                with sp.Fori(first[e], first[e + 1]) as k:
                    sp.wait_ge(xT_up, k + 1)
                    sp.wait_ge(idx_ok, k + 1)
                    i = nc.s_assert_within(k - first[e], 0, T - 1,
                                           skip_runtime_bounds_check_because="a group has at most all T tiles")
                    load(i * P + e * SEG, k)
            sp.wait_ge(xT_up, first[E] + 1)
            sp.dma_start(xs[:], seg[(E - 1) * SEG:(E - 1) * SEG + P, :]).then_inc(tile_in, 16)

        @block.gpsimd
        def _(pool):
            count = [0]

            def link(ins):
                count[0] += 1
                ins.then_inc(pool_step, 1)
                pool.wait_ge(pool_step, count[0])

            def keep(v, base, pattern, mult, fill=0.0):
                link(nc.gpsimd.affine_select(out=v, in_=v, compare_op=ALU.is_ge, fill=fill, base=base,
                                             pattern=pattern, channel_multiplier=mult))

            link(nc.gpsimd.memset(ident[:], 0.0))
            nc.gpsimd.affine_select(out=ident[:], in_=ident[:], compare_op=ALU.not_equal, fill=1.0, base=0,
                                    pattern=[[-1, P]], channel_multiplier=1).then_inc(ident_ok, 1)
            nc.gpsimd.memset(half[:, 0:1], -0.5)
            nc.gpsimd.memset(half[:, 1:2], EPS)
            nc.gpsimd.memset(group4[:], 1.0)
            link(nc.gpsimd.memset(blk16[:], 1.0))
            keep(blk16[:], 0, [[-HD, H]], 1)
            keep(blk16[:], HD - 1, [[HD, H]], -1)
            link(nc.gpsimd.tensor_tensor(slot4[:], blk16[:, 0:4], blk16[:, 4:8], ALU.add))
            link(nc.gpsimd.tensor_tensor(slot4[:], slot4[:], blk16[:, 8:12], ALU.add))
            link(nc.gpsimd.tensor_tensor(slot4[:], slot4[:], blk16[:, 12:16], ALU.add))
            keep(group4[:], 0, [[-W, 4]], 1)
            nc.gpsimd.affine_select(out=group4[:], in_=group4[:], compare_op=ALU.is_ge, fill=0.0, base=W - 1,
                                    pattern=[[W, 4]], channel_multiplier=-1).then_inc(heads_ok, 1)
            nc.gpsimd.memset(sel_l[:], 0.0)
            link(nc.gpsimd.memset(neg_l[:], 0.0))
            link(nc.gpsimd.memset(neg_l[W:2 * W, 1, 0:W], NEG))
            v = sel_l[0:W, :].rearrange("r (n q) -> r n q", q=W)
            link(nc.gpsimd.affine_select(out=v, in_=v, compare_op=ALU.not_equal, fill=1.0, base=0,
                                         pattern=[[0, BLK], [-1, W]], channel_multiplier=1))
            v = sel_l[W:2 * W, 0:W]
            link(nc.gpsimd.affine_select(out=v, in_=v, compare_op=ALU.not_equal, fill=1.0, base=0,
                                         pattern=[[-1, W]], channel_multiplier=1))
            keep(neg_l[0:W, :, :], -1, [[0, 2], [1, 2 * W]], -1, NEG)
            nc.gpsimd.affine_select(out=neg_l[0:W, :, :], in_=neg_l[0:W, :, :], compare_op=ALU.is_ge, fill=NEG, base=W,
                                    pattern=[[0, 2], [-1, 2 * W]], channel_multiplier=1).then_inc(masks_ok, 1)

            def latent_masks():
                nc.gpsimd.memset(neg_r[:], 0.0)
                link(nc.gpsimd.memset(sel_r[:], 0.0))
                link(nc.gpsimd.memset(sel_r[0:P // CH, :], 1.0))
                keep(sel_r[0:P // CH, :], 0, [[1, P]], -CH)
                keep(sel_r[0:P // CH, :], CH - 1, [[-1, P]], CH)
                nc.gpsimd.affine_select(
                    out=neg_r[0:P // CH, :, :], in_=neg_r[0:P // CH, :, :], compare_op=ALU.is_ge, fill=NEG, base=0,
                    pattern=[[P // CH, KT_], [-1, NL]], channel_multiplier=1).then_inc(masks_ok, 1)

            def routing_constants():
                nc.gpsimd.memset(ones[:], 1.0)
                link(nc.gpsimd.memset(before[:], 1.0))
                keep(before[:], -1, [[1, P]], -1)
                link(nc.gpsimd.memset(padrows[:], 0.0))
                link(nc.gpsimd.iota(padrows[:, D:XW].bitcast(I32), pattern=[[0, 1]], base=T * P, channel_multiplier=0))
                link(nc.gpsimd.iota(eint[:, 0:E], pattern=[[SEG, E]], base=0, channel_multiplier=0))
                link(nc.gpsimd.iota(eint[:, E:], pattern=[[1, E]], base=-3 * E, channel_multiplier=0))
                link(nc.gpsimd.tensor_copy(efl[:], eint[:]))
                link(nc.gpsimd.tensor_copy(nextrow[:], efl[:, 0:E]))
                link(nc.gpsimd.iota(x1[:, :, D].bitcast(I32), pattern=[[P, T]], base=0, channel_multiplier=1))

            def gate_columns():
                pool.wait_ge(g_in, 32)
                for q in range(2):
                    nc.gpsimd.tensor_scalar(gmat[:, q * H:(q + 1) * H], blk16[:], gcol[:, q:q + 1], None,
                                            ALU.mult).then_inc(gmat_ok, 1)

            def expand_k(b):
                pool.wait_ge(pj_free, pj[("K", b)] + 1)
                expand(nc.gpsimd, Kx[:, b % 2, :, W:], KT[:, b % 2, :], slot4[:], 4).then_inc(kx_done, 1)

            def expand_q(b):
                pool.wait_ge(pj_free, pj[("Q", b)] + 1)
                expand(nc.gpsimd, Qg[:, b % 2, :, :], QT[:, b % 2, :], group4[:], 4).then_inc(qg_done, 1)

            def expand_gk(b):
                pool.wait_ge(pj_free, pj[("G", b)] + 1)
                expand(nc.gpsimd, GKx[:, b % 2, :, :], GKs[:, b % 2, :], blk16[:, 0:LH], LH).then_inc(gk_done, 1)

            def layernorm(t):
                q = t % 2
                pool.wait_ge(stats, t + 1)
                link(nc.gpsimd.tensor_scalar(rstd[:, q, :], mv[:, q, 1:2], EPS, None, ALU.add))
                link(nc.gpsimd.tensor_tensor(rstd[:, q, :], rstd[:, q, :], half[:, 0:1], ALU.pow))
                nc.gpsimd.tensor_scalar(x1[:, t, 0:D], y[:, q, :], mv[:, q, 0:1], rstd[:, q, :],
                                        ALU.subtract, ALU.mult).then_inc(ln_done, 1)

            def scatter(b):
                pool.wait_ge(placed, b + 1)
                for t in range(b * KT_, (b + 1) * KT_):
                    pool.wait_ge(ln_done, t + 1)
                    nc.gpsimd.indirect_dma_start(seg, bass.IndirectOffsetOnAxis(ap=pos[:, t:t + 1], axis=0),
                                                 x1[:, t, :], None).then_inc(scattered, 16)

            pool.wait_ge(pj_free, pj[("Q", 0)] + 1)
            expand(nc.gpsimd, Qg[:, 0, :, 0:P], QT[:, 0, 0:P], group4[:], 4).then_inc(qg_done, 1)
            latent_masks()
            gate_columns()
            expand_gk(0)
            expand(nc.gpsimd, Qg[:, 0, :, P:], QT[:, 0, P:], group4[:], 4).then_inc(qg_done, 1)
            routing_constants()
            for t in range(T + 3):
                b, k = divmod(t, KT_)
                if t >= 3:
                    layernorm(t - 3)
                if b + 1 < NB and k < 3:
                    (expand_k, expand_q, expand_gk)[k](b + 1)
                if t == 1:
                    pool.wait_ge(b2_in, 16)
                    nc.gpsimd.tensor_tensor(b2s[:, 0:E - 1, :], b2r[:, 0:E - 1, :], b2r[:, 1:E, :],
                                            ALU.add).then_inc(b2_ok, 1)
                    nc.gpsimd.tensor_tensor(b2s[:, E - 1, :], b2r[:, E - 1, :], b2r[:, 0, :], ALU.add).then_inc(b2_ok, 1)
                if k == 0 and 2 <= b <= NB:
                    scatter(b - 2)
            scatter(NB - 1)

            first = load_table(pool, tile_table, range(E + 1), table_ok, T + E)
            ahead(pool, idx_ok, yo_ok, rs1, rs2, by=RING)

            def store(rows):
                nc.gpsimd.indirect_dma_start(
                    out.rearrange("b s d -> (b s) d"), bass.IndirectOffsetOnAxis(ap=idx[:], axis=0), rows, None,
                    bounds_check=T * P - 1, oob_is_err=False).then_inc(out_in, 16)

            link(nc.gpsimd.tensor_copy(idx[:], padrows[:, D:XW].bitcast(U32)))
            store(padrows[:, 0:D])
            for e in range(E):
                with pool.Fori(first[e], first[e + 1]) as k:
                    pool.wait_ge(bn2, k + 1)
                    nc.gpsimd.tensor_tensor(rstd2[:], mv2[:, 1:2], half[:, 1:2], ALU.add).then_inc(rs1, 1)
                    pool.wait_ge(rs1, k + 1 + RING)
                    nc.gpsimd.tensor_tensor(rstd2[:], rstd2[:], half[:, 0:1], ALU.pow).then_inc(rs2, 1)
                    pool.wait_ge(rs2, k + 1 + RING)
                    pool.wait_ge(out_in, k * 16 + 16)
                    nc.gpsimd.tensor_copy(idx[:], xk[:, bass.ds((k % RING) * XW + D, 1)].bitcast(U32)).then_inc(idx_ok, 1)
                    nc.gpsimd.tensor_scalar(yo[:], y2[:], mv2[:, 0:1], rstd2[:, 0:1],
                                            ALU.subtract, ALU.mult).then_inc(yo_ok, 1)
                    pool.wait_ge(table_ok, 1)
                    pool.wait_ge(idx_ok, k + 1 + RING)
                    pool.wait_ge(yo_ok, k + 1 + RING)
                    store(yo[:])
            pool.wait_ge(table_ok, 1)
            pool.wait_ge(out_in, first[E] * 16 + 16)

        @block.scalar
        def _(act):
            act.dma_start(wk_s[:], wk).then_inc(wk_in, 16)
            act.dma_start(wq_s[:], wq).then_inc(wq_in, 16)

            def take(use):
                kind, n = use
                act.wait_ge(pj_ready, pj[use] + 1)
                q = n % 2
                src = early_bank.get(use, bJ)
                if kind == "xT":
                    i = nc.scalar.copy(xT[:, q, W:], src[:])
                elif kind == "K":
                    i = nc.scalar.copy(KT[:, q, :], src[:])
                elif kind == "Q":
                    i = nc.scalar.copy(QT[:, q, :], src[:])
                elif kind == "GQ":
                    i = nc.scalar.copy(GQT[:, q, :], src[:])
                elif kind == "B":
                    i = nc.scalar.copy(b1c[:], bJ[:, 0:E * FC])
                elif kind == "R":
                    if n >= 1:
                        act.wait_ge(placed, n)
                    i = nc.scalar.copy(ranks[:].rearrange("p k e -> p (k e)"), bJ[:, 0:(KT_ + 1) * E])
                elif kind == "V":
                    if n >= 2:
                        act.wait_ge(pv_done, 3 * (n - 1))
                    for c in range(2):
                        h = slice(64 * c, 64 * c + 64)
                        i = nc.scalar.copy(Vx[h, q, :, :, c * HD:(c + 1) * HD],
                                           bJ[h, 0:BLK * D // 2].rearrange("p (n a d) -> p n a d", n=BLK, d=HD))
                else:
                    nc.scalar.mul(GKs[:, q, :], src[:, 0:NL], 1.0 / CH)
                    for c in range(2):
                        h = slice(64 * c, 64 * c + 64)
                        nc.scalar.mul(GVx[h, q, :, c * HD:(c + 1) * HD],
                                      src[h, NL:NL + LD // 2].rearrange("p (a d) -> p a d", d=HD),
                                      1.0 / CH)
                    i = nc.scalar.activation(gex[:, q, :, :],
                                             src[:, P:P + KT_ * 2 * H].rearrange("p (k g) -> p k g", k=KT_),
                                             ACT.Exp, scale=-1.0)
                i.then_inc(pj_free, 1)

            def exp(t, j):
                act.wait_ge(shifted, 3 * t + j + 1)
                v = Pr[:, t % 2, j, :]
                nc.scalar.activation(v, v, ACT.Exp, scale=SCALE).then_inc(exped, 1)

            def turned_copy(t, j):
                u = 3 * t + j
                act.wait_ge(turned, u + 1)
                if t >= 1:
                    act.wait_ge(pv_done, u - 2)
                nc.scalar.copy(PTs[:, j, :, :], bT[u % 2][:].rearrange("p (c q) -> p c q", c=4)).then_inc(turned_out, 1)

            act.wait_ge(ident_ok, 1)
            nc.scalar.activation(warm[:], ident[0:1, 0:1], ACT.Exp)
            act.wait_ge(vconst_ok, 1)
            for use in first_uses:
                take(use)
            for t in range(T + 3):
                for j in range(2):
                    if 1 <= t <= T:
                        turned_copy(t - 1, j)
                if t >= 3:
                    act.wait_ge(attT_up, t - 2)
                    nc.scalar.copy(attT[:], aT).then_inc(attT_out, 1)
                if t < T:
                    take(("V", t))
                    for use in early_uses if t == 0 else []:
                        take(use)
                    exp(t, 0)
                    exp(t, 1)
                if 1 <= t <= T:
                    turned_copy(t - 1, 2)
                if 2 <= t < T + 2:
                    act.wait_ge(remT_up, t - 1)
                    nc.scalar.copy(remT[:], rT).then_inc(remT_out, 1)
                for use in others(t):
                    take(use)
                if t < T:
                    exp(t, 2)
            take(("R", NB - 1))

            pad_tails(act, range(1, E, 2))
            first = load_table(act, tile_table, range(E + 1), table_ok, T + E)
            ahead(act, relu_a)
            for e in range(E):
                with act.Fori(first[e], first[e + 1]) as k:
                    act.wait_ge(up_a, k + 1)
                    act.wait_ge(down, k + 1)
                    for c in range(FC):
                        nc.scalar.activation(ha[:, c, :], bA[:, c * P:(c + 1) * P], ACT.Relu,
                                             bias=b1c[:, e * FC + c:e * FC + c + 1]).then_inc(relu_a, 1)

        @block.vector
        def _(dve):
            count = [0]

            def link(ins):
                count[0] += 1
                ins.then_inc(dve_step, 1)
                dve.wait_ge(dve_step, count[0])

            nc.vector.memset(xT[:, :, 0:W], 0.0)
            nc.vector.memset(Kx[:, :, :, 0:W], 0.0)
            for v in (wgq_s[:, LD:], wgk_s[:, LD:], rout_s[LD:, :], rem[:, :, LD:], GVx[:]):
                nc.vector.memset(v, 0.0)
            link(nc.vector.memset(Vx[:], 0.0))
            for c in range(2):
                h = slice(64 * c, 64 * c + 64)
                nc.vector.memset(Vx[h, :, :, :, 2 * HD + c:2 * HD + c + 1], 1.0)
                last = nc.vector.memset(GVx[h, :, :, 2 * HD + c:2 * HD + c + 1], 1.0)
            last.then_inc(vconst_ok, 1)

            def pooled(b):
                dve.wait_ge(pj_free, pj[("xT", b)] + 1)
                nc.vector.tensor_reduce(xp[:, b % 2, :], xT[:, b % 2, W:].rearrange("p (n c) -> p n c", c=CH),
                                        AX.X, ALU.add).then_inc(xp_done, 1)

            def gates(b):
                dve.wait_ge(pj_free, pj[("G", b)] + 1)
                g = gat[:, b % 2, :, :]
                link(nc.vector.tensor_scalar(g, gex[:, b % 2, :, :], 1.0, None, ALU.add))
                link(nc.vector.reciprocal(g, g))

            def shift(t, j):
                u = 3 * t + j
                dve.wait_ge(scores, u + 1)
                s = bS[j][:].rearrange("p (h k) -> p h k", h=8)
                link(nc.vector.tensor_reduce(mx[:, j, :], s, AX.X, ALU.max))
                if t >= 2:
                    dve.wait_ge(turned, u - 5)
                nc.vector.tensor_tensor(Pr[:, t % 2, j, :].rearrange("p (h k) -> p h k", h=8), s,
                                        mx[:, j, :].unsqueeze(2).to_broadcast([P, 8, 2 * W]),
                                        ALU.subtract).then_inc(shifted, 1)

            def normalise(t):
                q, b, k = t % 2, t // KT_, t % KT_
                dve.wait_ge(pv_done, 3 * t + 3)
                pv = bV[:, 0:(HP + LP) * PW].rearrange("p (a c) -> p a c", c=PW)
                link(nc.vector.reciprocal(rs[:, q, :, :], pv[:, :, 2 * HD:]))
                link(nc.vector.tensor_tensor(grs[:, q, :], rs[:, q, 0:HP, :].rearrange("p a c -> p (a c)"),
                                             gat[:, b % 2, k, 0:H], ALU.mult))
                nc.vector.tensor_tensor(
                    loc[:, q, :].rearrange("p (a c d) -> p a c d", c=2, d=HD),
                    pv[:, 0:HP, 0:2 * HD].rearrange("p a (c d) -> p a c d", c=2),
                    grs[:, q, :].rearrange("p (a c) -> p a c", c=2).unsqueeze(3).to_broadcast([P, HP, 2, HD]), ALU.mult)
                nc.vector.tensor_tensor(
                    rem[:, q, 0:LD].rearrange("p (a c d) -> p a c d", c=2, d=HD),
                    pv[:, HP:, 0:2 * HD].rearrange("p a (c d) -> p a c d", c=2),
                    rs[:, q, HP:, :].unsqueeze(3).to_broadcast([P, LP, 2, HD]), ALU.mult).then_inc(normed, 1)

            def gate(t):
                q, b, k = t % 2, t // KT_, t % KT_
                dve.wait_ge(rem_up, t + 1)
                if t >= 1:
                    dve.wait_ge(attT_up, t)
                link(nc.vector.tensor_tensor(
                    att0[:].rearrange("p (h d) -> p h d", d=HD), rM.rearrange("p (h d) -> p h d", d=HD),
                    gat[:, b % 2, k, H:].unsqueeze(2).to_broadcast([P, H, HD]), ALU.mult))
                nc.vector.tensor_tensor(att[:], att0[:], loc[:, q, :], ALU.add).then_inc(gated, 1)

            def residual(t):
                q = t % 2
                dve.wait_ge(proj_up, t + 1)
                if t >= 2:
                    dve.wait_ge(ln_done, t - 1)
                ins = nc.vector.tensor_tensor(y[:, q, :], wO, x_tok[:, t, :], ALU.add)
                ins.then_inc(summed, 1)
                dve.wait_ge(summed, t + 1)
                link(nc.vector.bn_stats(st[:, q, :], y[:, q, :]))
                nc.vector.bn_aggr(mv[:, q, :], st[:, q, :]).then_inc(stats, 1)

            def mark(b):
                dve.wait_ge(ln_done, (b + 1) * KT_)
                v = x1[:, b * KT_:(b + 1) * KT_, :]
                link(nc.vector.tensor_tensor(tsum[:], v[:, :, 0], v[:, :, 1], ALU.add))
                link(nc.vector.tensor_scalar(near[:], tsum[:], ROUND, -ROUND, ALU.add, ALU.add))
                link(nc.vector.tensor_tensor(off[:], near[:], tsum[:], ALU.subtract))
                nc.vector.tensor_scalar(over[:], off[:], 0.0, None, ALU.is_gt)
                link(nc.vector.tensor_scalar(frac[:], off[:], 0.0, None, ALU.not_equal))
                link(nc.vector.tensor_tensor(near[:], near[:], over[:], ALU.subtract))
                link(nc.vector.scalar_tensor_tensor(frac[:], tsum[:], 0.0, frac[:], ALU.is_lt, ALU.mult))
                link(nc.vector.tensor_tensor(near[:], near[:], frac[:], ALU.add))
                link(nc.vector.tensor_scalar(off[:], near[:], 1.0 / E, 3.0 - 0.5 + 0.5 / E, ALU.mult, ALU.add))
                link(nc.vector.tensor_scalar(off[:], off[:], ROUND, -ROUND, ALU.add, ALU.add))
                link(nc.vector.scalar_tensor_tensor(near[:], off[:], -float(E), near[:], ALU.mult, ALU.add))
                nc.vector.tensor_tensor(onehot[:], near[:].unsqueeze(2).to_broadcast([P, KT_, E]),
                                        efl[:, E:].unsqueeze(1).to_broadcast([P, KT_, E]),
                                        ALU.is_equal).then_inc(marked, 1)

            def place(b):
                dve.wait_ge(marked, b + 1)
                dve.wait_ge(pj_free, pj[("R", b)] + 1)
                link(nc.vector.tensor_tensor(cand[:], ranks[:, 0:KT_, :],
                                             nextrow[:].unsqueeze(1).to_broadcast([P, KT_, E]), ALU.add))
                link(nc.vector.tensor_tensor(cand[:], cand[:], onehot[:], ALU.mult))
                link(nc.vector.tensor_reduce(posf[:], cand[:], AX.X, ALU.add))
                link(nc.vector.tensor_tensor(nextrow[:], nextrow[:], ranks[:, KT_, :], ALU.add))
                nc.vector.tensor_copy(pos[:, b * KT_:(b + 1) * KT_], posf[:]).then_inc(placed, 1)
                if b == NB - 1:
                    nc.vector.tensor_copy(tail_table[:], nextrow[0:1, :]).then_inc(tails_ok, 1)

            def count_tiles():
                n, m = tiles[:, 0, :], tiles[:, 1, :]
                link(nc.vector.memset(tiles[:], 0.0))
                link(nc.vector.tensor_tensor(m[:, 1:], nextrow[0:1, :], efl[0:1, 0:E], ALU.subtract))
                link(nc.vector.tensor_scalar(m[:, 1:], m[:, 1:], 1.0 / P, 0.5 - 0.5 / P, ALU.mult, ALU.add))
                link(nc.vector.tensor_scalar(m[:, 1:], m[:, 1:], ROUND, -ROUND, ALU.add, ALU.add))
                link(nc.vector.tensor_scalar(n[:, 1:], m[:, 1:], 1.0, None, ALU.max))
                src, dst, d = n, m, 1
                while d <= E:
                    link(nc.vector.tensor_copy(dst[:, 0:d], src[:, 0:d]))
                    link(nc.vector.tensor_tensor(dst[:, d:], src[:, d:], src[:, 0:E + 1 - d], ALU.add))
                    src, dst, d = dst, (tiles[:, 2, :] if dst is m else m), 2 * d
                nc.vector.tensor_copy(tile_table[:], src).then_inc(table_ok, 1)

            pooled(0)
            dve.wait_ge(pj_free, pj[("K", 0)] + 1)
            dve.wait_ge(heads_ok, 1)
            for o in (slice(0, P), slice(P, S)):
                expand(nc.vector, Kx[:, 0, :, W + o.start:W + o.stop], KT[:, 0, o], slot4[:], 4).then_inc(kx_done, 1)
            for t in range(T + 3):
                b, k = divmod(t, KT_)
                if 2 <= t < T + 2:
                    normalise(t - 2)
                if t < T:
                    shift(t, 0)
                    if k == 1 and b + 1 < NB:
                        pooled(b + 1)
                    shift(t, 1)
                    if t == 0:
                        gates(0)
                    if k == 3 and b + 1 < NB:
                        gates(b + 1)
                if t >= 3:
                    residual(t - 3)
                if t < T:
                    shift(t, 2)
                if 2 <= t < T + 2:
                    gate(t - 2)
                if k == 3 and 1 <= b < NB:
                    mark(b - 1)
                if k == 0 and 2 <= b <= NB:
                    place(b - 2)
            mark(NB - 1)
            place(NB - 1)
            count_tiles()

            dve.wait_ge(b2_ok, 2)
            first = load_table(dve, tile_table, range(E + 1), table_ok, T + E)

            def column_copy(k):
                dve.wait_ge(xT_up, k + 2)
                dve.wait_ge(up_b, k + 1)
                nc.vector.tensor_copy(xsT[:], bX[:, 0:P]).then_inc(xT_out, 1)

            ahead(dve, xT_out, relu_b, biased, y_ok)
            column_copy(0)
            for e in range(E):
                a = (e + 1) % E
                with dve.Fori(first[e], first[e + 1]) as k:
                    dve.wait_ge(up_b, k + 2)
                    dve.wait_ge(down, k + 1)
                    for c in range(FC):
                        nc.vector.tensor_scalar(hb[:, c, :], bB[:, c * P:(c + 1) * P], b1c[:, a * FC + c:a * FC + c + 1],
                                                0.0, ALU.add, ALU.max).then_inc(relu_b, 1)
                    column_copy(k + 1)
                    dve.wait_ge(down, k + 2)
                    nc.vector.tensor_tensor(ysum[:], bY[:, 0:D], b2s[:, e, :], ALU.add).then_inc(biased, 1)
                    dve.wait_ge(biased, k + 2)
                    dve.wait_ge(kept, k * 16 + 16)
                    dve.wait_ge(yo_ok, k + RING)
                    nc.vector.scalar_tensor_tensor(y2[:], ysum[:], 0.5, xk[:, bass.ds((k % RING) * XW, D)],
                                                   ALU.mult, ALU.add).then_inc(y_ok, 1)
                    dve.wait_ge(y_ok, k + 2)
                    nc.vector.bn_stats(st2[:], y2[:]).then_inc(bn1, 1)
                    dve.wait_ge(table_ok, 1)
                    dve.wait_ge(bn1, k + 1)
                    nc.vector.bn_aggr(mv2[:], st2[:]).then_inc(bn2, 1)

        @block.tensor
        def _(pe):
            mm = nc.tensor.matmul

            def half_heads(w, c):
                return w[:].rearrange("p (a c d) -> p a c d", c=2, d=HD)[:, :, c, :]

            def fill(use):
                kind, n = use
                if use in early_bank:
                    pe.wait_ge(pj_free, pj[("xT", 0)] + 1)
                elif use == ("V", 0):
                    pe.wait_ge(pj_free, pj[("xT", 0)] + 1)
                elif pj[use] >= 1:
                    pe.wait_ge(pj_free, pj[use])
                q = n % 2
                dst = early_bank.get(use, bJ)
                if kind == "xT":
                    pe.wait_ge(x_in[n], 16)
                    for i in range(KT_):
                        last = nc.tensor.transpose(bJ[:, i * P:(i + 1) * P], x_tok[:, n * KT_ + i, :], ident[:])
                elif kind == "K":
                    if n == 0:
                        pe.wait_ge(wk_in, 16)
                    last = mm(dst[:], wk_s[:], xT[:, q, W:], start=True, stop=True)
                elif kind == "Q":
                    if n == 0:
                        pe.wait_ge(wq_in, 16)
                    last = mm(dst[:], wq_s[:], xT[:, q, W:], start=True, stop=True)
                elif kind == "GQ":
                    if n == 0:
                        pe.wait_ge(wgq_in, 16)
                    last = mm(dst[:], wgq_s[:], xT[:, q, W:], start=True, stop=True)
                elif kind == "B":
                    pe.wait_ge(b_in, 16)
                    last = nc.tensor.transpose(bJ[:, 0:E * FC], b1r[:], ident[0:E * FC, 0:E * FC])
                elif kind == "R":
                    pe.wait_ge(marked, n + 1)
                    oh = onehot[:].rearrange("p k e -> p (k e)")
                    mm(bJ[:, 0:KT_ * E], before[:], oh, start=True, stop=False, skip_group_check=True)
                    for i in range(1, KT_ + 1):
                        last = mm(bJ[:, i * E:(KT_ + 1) * E], ones[:], oh[:, 0:(KT_ + 1 - i) * E], start=False,
                                  stop=(i == KT_), skip_group_check=True)
                elif kind == "G":
                    pe.wait_ge(xp_done, n + 1)
                    if n == 0:
                        pe.wait_ge(wg_in, 32)
                        pe.wait_ge(gmat_ok, 2)
                        pe.wait_ge(pj_free, pj[("Q", 0)] + 1)
                    mm(dst[:, 0:NL], wgk_s[:], xp[:, q, :], start=True, stop=True)
                    for r in range(BLK):
                        mm(dst[r * W:(r + 1) * W, NL:NL + LD // 2], xp[:, q, (r % 2) * W:(r % 2 + 1) * W],
                           half_heads(wgv_s, r // 2), start=True, stop=True)
                    for i in range(KT_):
                        last = mm(dst[:, P + i * 2 * H:P + (i + 1) * 2 * H], QT[:, q, i * P:(i + 1) * P], gmat[:],
                                  start=True, stop=True)
                else:
                    b, k = divmod(n, KT_)
                    for i in range(BLK):
                        o = k * P + i * W
                        for r in range(BLK):
                            w = o + (r % 2) * W
                            last = mm(bJ[r * W:(r + 1) * W, i * D // 2:(i + 1) * D // 2], xT[:, b % 2, w:w + W],
                                      half_heads(wv_s, r // 2), start=True, stop=True)
                last.then_inc(pj_ready, 1)

            def mask(t, j):
                if t == 0 and j != 1:
                    pe.wait_ge(masks_ok, 1 + j // 2)
                if t >= 1:
                    pe.wait_ge(shifted, 3 * t + j - 2)
                k = t % KT_
                if j < 2:
                    sel, neg = sel_l, neg_l[:, 1 if k == 0 else 0, :]
                else:
                    sel, neg = sel_r, neg_r[:, k, :]
                mm(bS[j][:], sel[:], neg.unsqueeze(1).to_broadcast([P, 8, 2 * W]),
                   start=True, stop=False, skip_group_check=True)

            def score_local(t, j):
                b, k = divmod(t, KT_)
                q = b % 2
                if t <= 1 and j == 0:
                    pe.wait_ge(kx_done, t + 1)
                    pe.wait_ge(qg_done, t + 1)
                elif k == 0 and j == 0:
                    pe.wait_ge(kx_done, b + 2)
                    pe.wait_ge(qg_done, b + 2)
                for g in range(2):
                    for i in range(BLK):
                        o = k * P + i * W
                        last = mm(bS[j][i * W:(i + 1) * W, g * 256:(g + 1) * 256],
                                  Qg[:, q, 2 * j + g, o:o + W], Kx[:, q, :, o:o + 2 * W],
                                  start=False, stop=(g == 1), skip_group_check=True)
                last.then_inc(scores, 1)

            def score_latent(t):
                b, k = divmod(t, KT_)
                if k == 0:
                    pe.wait_ge(gk_done, b + 1)
                mm(bS[2][:], GQT[:, b % 2, k * P:(k + 1) * P], GKx[:, b % 2, :, :].rearrange("p h n -> p (h n)"),
                   start=False, stop=True, skip_group_check=True).then_inc(scores, 1)

            def turn(t, j):
                u = 3 * t + j
                pe.wait_ge(exped, u + 1)
                if u >= 2:
                    pe.wait_ge(turned_out, u - 1)
                for c in range(4):
                    last = nc.tensor.transpose(bT[u % 2][:, c * P:(c + 1) * P], Pr[:, t % 2, j, c * P:(c + 1) * P], ident[:])
                last.then_inc(turned, 1)

            def weigh(t, j):
                u, q = 3 * t + j, t % 2
                pe.wait_ge(turned_out, u + 1)
                if j == 0:
                    pe.wait_ge(pj_free, pj[("V", t)] + 1)
                    if t >= 1:
                        pe.wait_ge(normed, t)
                for c in range(4):
                    a = 4 * j + c
                    if j < 2:
                        for i in range(BLK):
                            last = mm(bV[i * W:(i + 1) * W, a * PW:(a + 1) * PW], PTs[:, j, c, i * W:(i + 1) * W],
                                      Vx[:, q, i, a, :], start=True, stop=True)
                    else:
                        last = mm(bV[:, a * PW:(a + 1) * PW], PTs[:, j, c, :], GVx[:, (t // KT_) % 2, c, :],
                                  start=True, stop=True)
                last.then_inc(pv_done, 1)

            pe.wait_ge(ident_ok, 1)
            pe.wait_ge(vconst_ok, 1)
            for use in first_uses:
                fill(use)
            for t in range(T + 3):
                for j in range(2):
                    if t < T:
                        mask(t, j)
                    if 1 <= t <= T:
                        turn(t - 1, j)
                if t >= 3:
                    pe.wait_ge(gated, t - 2)
                    nc.tensor.transpose(aT, att[:], ident[:]).then_inc(attT_up, 1)
                if t < T:
                    if t == 0:
                        pe.wait_ge(wv_in, 16)
                    fill(("V", t))
                    score_local(t, 0)
                    score_local(t, 1)
                    for use in early_uses if t == 0 else []:
                        fill(use)
                if 1 <= t <= T:
                    weigh(t - 1, 0)
                    weigh(t - 1, 1)
                if t >= 3:
                    pe.wait_ge(attT_out, t - 2)
                    mm(wO, attT[:], wout_s[:], start=True, stop=True).then_inc(proj_up, 1)
                if t < T:
                    mask(t, 2)
                    score_latent(t)
                if 1 <= t <= T:
                    turn(t - 1, 2)
                if 2 <= t < T + 2:
                    pe.wait_ge(normed, t - 1)
                    if t >= 3:
                        pe.wait_ge(summed, t - 2)
                    nc.tensor.transpose(rT, rem[:, t % 2, :], ident[:]).then_inc(remT_up, 1)
                for use in others(t)[0:1]:
                    fill(use)
                if 1 <= t <= T:
                    weigh(t - 1, 2)
                if 2 <= t < T + 2:
                    if t == 2:
                        pe.wait_ge(wo_in, 32)
                    pe.wait_ge(remT_out, t - 1)
                    mm(rM, remT[:], rout_s[:], start=True, stop=True).then_inc(rem_up, 1)
                for use in others(t)[1:]:
                    fill(use)
            fill(("R", NB - 1))

            pe.wait_ge(f_in, 32)
            first = load_table(pe, tile_table, range(E + 1), table_ok, T + E)

            def columns(k):
                pe.wait_ge(tile_in, (k + 1) * 16)
                pe.wait_ge(xT_out, k + 1)
                nc.tensor.transpose(bX[:, 0:P], xs[:, 0:D], ident[:]).then_inc(xT_up, 1)

            ahead(pe, xT_up, up_b, down)
            columns(0)
            for e in range(E):
                a = (e + 1) % E
                with pe.Fori(first[e], first[e + 1]) as k:
                    pe.wait_ge(xT_out, k + 2)
                    pe.wait_ge(relu_a, k * FC + 1)
                    for c in range(FC):
                        last = mm(bA[:, c * P:(c + 1) * P], w1_s[:, e, c * P:(c + 1) * P], xsT[:], start=True, stop=True)
                    last.then_inc(up_a, 1)
                    pe.wait_ge(relu_b, k * FC + 1)
                    for c in range(FC):
                        last = mm(bB[:, c * P:(c + 1) * P], w1_s[:, a, c * P:(c + 1) * P], xsT[:], start=True, stop=True)
                    last.then_inc(up_b, 1)
                    pe.wait_ge(biased, k + 1)
                    for c in range(FC):
                        pe.wait_ge(relu_a, k * FC + c + 2)
                        mm(bY[:, 0:D], ha[:, c, :], w2_s[:, e, c, :], start=(c == 0), stop=False)
                    columns(k + 1)
                    for c in range(FC):
                        pe.wait_ge(relu_b, k * FC + c + 2)
                        last = mm(bY[:, 0:D], hb[:, c, :], w2_s[:, a, c, :], start=False, stop=(c == FC - 1))
                    last.then_inc(down, 1)


_INS = ["L0_attn_x", "L0_attn_wq", "L0_attn_wk", "L0_attn_wv", "L0_attn_wgq", "L0_attn_wgk", "L0_attn_wgv",
        "L0_attn_r_out_w", "L0_attn_gate_local_w", "L0_attn_gate_remote_w", "L0_attn_w_out",
        "L0_ffn_W1", "L0_ffn_b1", "L0_ffn_W2", "L0_ffn_b2"]


def kernel(**inputs):
    import numpy as _np
    import concourse.bacc as _bacc
    from concourse import mybir as _mybir
    from concourse.bass_utils import run_bass_kernel_spmd as _run

    nc = _bacc.Bacc("TRN2", target_bir_lowering=False, num_devices=1)
    arrays, args = {}, []
    for name in _INS:
        a = _np.ascontiguousarray(inputs[name])
        arrays[f"in_{name}"] = a
        args.append(nc.dram_tensor(f"in_{name}", a.shape, _mybir.dt.from_np(a.dtype), kind="ExternalInput").ap())
    shape = inputs["L0_attn_x"].shape
    args.append(nc.dram_tensor("out0", shape, F32, kind="ExternalOutput").ap())
    n = shape[0] * shape[1]
    experts = inputs["L0_ffn_W1"].shape[0]
    args.append(nc.dram_tensor("groups", (experts * (n + P), P + 1), F32, kind="Internal").ap())
    bass_windowed_latent_attention_hash_moe(nc, *args)
    r = _run(nc, [arrays], core_ids=[0])
    return r.results[0]["out0"]
```

```python
from contextlib import ExitStack

import concourse.bass as bass
from concourse import mybir

ALU = mybir.AluOpType
ACT = mybir.ActivationFunctionType
AX = mybir.AxisListType
F32 = mybir.dt.float32
BF16 = mybir.dt.bfloat16
I32 = mybir.dt.int32
U32 = mybir.dt.uint32

P = 128
NEG = -1.0e30
ROUND = 12582912.0


def bass_windowed_latent_attention_hash_moe(
    nc, x, wq, wk, wv, wgq, wgk, wgv, r_out_w, gate_l, gate_r, w_out, W1, b1, W2, b2, out, seg,
):
    NB, S, D = x.shape
    H, HD = gate_l.shape
    LD = wgq.shape[1]
    LH = LD // HD
    W = 32
    NL = 64
    CH = S // NL
    E, _, F = W1.shape
    FC = F // P
    KT_ = S // P
    T = NB * KT_
    BLK = P // W
    HP = H // 2
    LP = LH // 2
    PW = 2 * HD + 2
    SCALE = float(HD) ** -0.5
    EPS = 1e-5
    SEG = seg.shape[0] // E
    BA = FC // 2
    RING = 4
    XW = D + 1

    with ExitStack() as ctx:
        def sb(name, shape, dt=F32):
            return ctx.enter_context(nc.sbuf_tensor(name, shape, dt))

        def bank(name, dt=F32):
            return ctx.enter_context(nc.psum_tensor(name, [P, 512], dt))

        def sem(name):
            return ctx.enter_context(nc.semaphore(name))

        x_tok = sb("x_tok", [P, T, D])
        wq_s, wk_s, wv_s, wout_s = (sb(n, [P, P]) for n in ("wq_s", "wk_s", "wv_s", "wout_s"))
        wgq_s, wgk_s = (sb(n, [P, P]) for n in ("wgq_s", "wgk_s"))
        wgv_s = sb("wgv_s", [P, LD])
        rout_s = sb("rout_s", [P, P])
        gcol = sb("gcol", [P, 2])
        ident = sb("ident", [P, P])
        warm = sb("warm", [1, 1])
        half = sb("half", [P, 2])
        blk16 = sb("blk16", [P, H])
        slot4 = sb("slot4", [P, 4])
        group4 = sb("group4", [P, 4])
        gmat = sb("gmat", [P, 2 * H])
        sel_l = sb("sel_l", [P, P], BF16)
        neg_l = sb("neg_l", [P, 2, 2 * W], BF16)
        sel_r = sb("sel_r", [P, P], BF16)
        neg_r = sb("neg_r", [P, KT_, NL], BF16)

        xT = sb("xT", [P, 2, W + S])
        KT = sb("KT", [P, 2, S])
        QT = sb("QT", [P, 2, S])
        Kx = sb("Kx", [P, 2, 4, W + S])
        Qg = sb("Qg", [P, 2, 4, S])
        xp = sb("xp", [P, 2, NL])
        GQT = sb("GQT", [P, 2, S])
        GKs = sb("GKs", [P, 2, NL])
        GKx = sb("GKx", [P, 2, LH, NL])
        GVx = sb("GVx", [P, 2, LP, PW])
        gex = sb("gex", [P, 2, KT_, 2 * H])
        gat = sb("gat", [P, 2, KT_, 2 * H])
        Vx = sb("Vx", [P, 2, BLK, HP, PW])
        Pr = sb("Pr", [P, 2, 3, 512])
        PTs = sb("PTs", [P, 3, 4, P])
        mx = sb("mx", [P, 3, 8])
        rs = sb("rs", [P, 2, HP + LP, 2])
        grs = sb("grs", [P, 2, H])
        loc = sb("loc", [P, 2, D])
        rem = sb("rem", [P, 2, P])
        remT = sb("remT", [P, P])
        att0 = sb("att0", [P, D])
        att = sb("att", [P, D])
        attT = sb("attT", [P, P])
        y = sb("y", [P, 2, D])
        st = sb("st", [P, 2, 6])
        mv = sb("mv", [P, 2, 2])
        rstd = sb("rstd", [P, 2, 1])
        x1 = sb("x1", [P, T, XW])

        before = sb("before", [P, P], BF16)
        ones = sb("ones", [P, P], BF16)
        eint = sb("eint", [P, 2 * E], I32)
        efl = sb("efl", [P, 2 * E])
        tsum = sb("tsum", [P, KT_])
        near = sb("near", [P, KT_])
        off = sb("off", [P, KT_])
        over = sb("over", [P, KT_])
        frac = sb("frac", [P, KT_])
        onehot = sb("onehot", [P, KT_, E], BF16)
        ranks = sb("ranks", [P, KT_ + 1, E])
        nextrow = sb("nextrow", [P, E])
        cand = sb("cand", [P, KT_, E])
        posf = sb("posf", [P, KT_])
        pos = sb("pos", [P, T], U32)
        padrows = sb("padrows", [P, XW])
        Z = E
        tiles = sb("tiles", [1, 4, Z + E + 1])
        tail_table = sb("tail_table", [1, E], I32)
        tile_table = sb("tile_table", [1, E + 1], I32)

        w1_s = sb("w1_s", [P, E, F])
        w2_s = sb("w2_s", [P, E, FC, D])
        b1r = sb("b1r", [E * FC, P])
        b1c = sb("b1c", [P, E * FC])
        b2r = sb("b2r", [P, E, D])
        b2s = sb("b2s", [P, E, D])
        xs = sb("xs", [P, XW])
        xk = sb("xk", [P, RING * XW])
        xsT = sb("xsT", [P, P])
        ha = sb("ha", [P, FC, P])
        hb = sb("hb", [P, FC, P])
        ysum = sb("ysum", [P, D])
        y2 = sb("y2", [P, D])
        st2 = sb("st2", [P, 6])
        mv2 = sb("mv2", [P, 2])
        rstd2 = sb("rstd2", [P, 1])
        yo = sb("yo", [P, D])
        idx = sb("idx", [P, 1], U32)


        bS = [bank(f"bS{j}") for j in range(3)]
        bT = [bank(f"bT{j}") for j in range(2)]
        bV = bank("bV")
        bJ = bank("bJ")
        bL = bank("bL")
        rT, rM, aT, wO = (bL[:, i * P:(i + 1) * P] for i in range(4))

        bA, bB, bX, bY, bC = bS[0], bS[1], bS[2], bV, bT[0]

        x_in = [sem(f"x_in{b}") for b in range(NB)]
        wk_in, wq_in, wgq_in, wg_in, wv_in, wo_in, g_in = (
            sem(n) for n in ("wk_in", "wq_in", "wgq_in", "wg_in", "wv_in", "wo_in", "g_in"))
        gmat_ok = sem("gmat_ok")
        ident_ok = sem("ident_ok")
        heads_ok = sem("heads_ok")
        masks_ok = sem("masks_ok")
        vconst_ok = sem("vconst_ok")
        pj_ready = sem("pj_ready")
        pj_free = sem("pj_free")
        kx_done = sem("kx_done")
        qg_done = sem("qg_done")
        gk_done = sem("gk_done")
        xp_done = sem("xp_done")
        gat_done = sem("gat_done")
        scores = sem("scores")
        shifted = sem("shifted")
        exped = sem("exped")
        turned = sem("turned")
        turned_out = sem("turned_out")
        pv_done = sem("pv_done")
        normed = sem("normed")
        remT_up = sem("remT_up")
        remT_out = sem("remT_out")
        rem_up = sem("rem_up")
        gated = sem("gated")
        attT_up = sem("attT_up")
        attT_out = sem("attT_out")
        proj_up = sem("proj_up")
        summed = sem("summed")
        stats = sem("stats")
        ln_done = sem("ln_done")
        rstd_ok = sem("rstd_ok")
        dve_step = sem("dve_step")
        pool_step = sem("pool_step")
        marked = sem("marked")
        placed = sem("placed")
        scattered = sem("scattered")
        pad_ok = sem("pad_ok")
        padded = sem("padded")
        tails_ok = sem("tails_ok")
        table_ok = sem("table_ok")
        f_in = sem("f_in")
        b_in = sem("b_in")
        b2_in = sem("b2_in")
        b2_ok = sem("b2_ok")
        tile_in = sem("tile_in")
        kept = sem("kept")
        xT_up = sem("xT_up")
        xT_out = sem("xT_out")
        up_a = sem("up_a")
        up_b = sem("up_b")
        relu_a = sem("relu_a")
        relu_b = sem("relu_b")
        down = sem("down")
        biased = sem("biased")
        y_ok = sem("y_ok")
        bn1 = sem("bn1")
        bn2 = sem("bn2")
        yo_ok = sem("yo_ok")
        out_in = sem("out_in")
        rs1 = sem("rs1")
        rs2 = sem("rs2")
        idx_ok = sem("idx_ok")

        chunks = [range(b * KT_, (b + 1) * KT_) for b in range(NB - 1)] + [range(T - KT_, T - 2), range(T - 2, T)]

        def others(t):
            b, k = divmod(t, KT_)
            u = []
            if b + 1 < NB:
                u += {0: [("xT", b + 1), ("K", b + 1)], 1: [("Q", b + 1), ("GQ", b + 1)], 2: [("G", b + 1)], 3: []}[k]
            if k == 0 and 2 <= b <= NB:
                u.append(("R", b - 2))
            if t == T + 2:
                u.append(("R", NB - 1))
            if t == 2:
                u.append(("B", 0))
            return u

        first_uses = [(n, 0) for n in ("xT", "K", "Q")]
        early_uses = [(n, 0) for n in ("GQ", "G")]
        pj = {}
        for use in (first_uses + [("V", 0)] + early_uses + others(0)
                    + [u for t in range(1, T + 3) for u in [("V", t)] * (t < T) + others(t)] + [("R", NB)]):
            pj[use] = len(pj)
        early_bank = {("K", 0): bT[0], ("Q", 0): bT[1], ("GQ", 0): bV, ("G", 0): bL}

        block = ctx.enter_context(nc.Block())

        def load_table(eng, tab, entries, ready, most):
            eng.wait_ge(ready, 1)
            return [eng.value_load(tab[0:1, i:i + 1], min_val=0, max_val=most) for i in entries]

        def expand(eng, dst, src, mask, n):
            return eng.tensor_tensor(
                dst, src.unsqueeze(1).to_broadcast([src.shape[0], n, src.shape[1]]),
                mask.unsqueeze(2).to_broadcast([src.shape[0], n, src.shape[1]]), ALU.mult)

        def ahead(eng, *sems, by=1):
            for s in sems:
                eng.sem_inc(s, by)

        @block.sync
        def _(sp):
            xr = x.rearrange("b (k p) d -> b p k d", p=P)
            def load_x(b):
                sp.dma_start(x_tok[:, b * KT_:(b + 1) * KT_, :], xr[b]).then_inc(x_in[b], 16)

            load_x(0)
            for dst, src, s in ((wv_s[:], wv, wv_in), (wgq_s[:, 0:LD], wgq, wgq_in),
                                (gcol[:, 0:1], gate_l.rearrange("h (d a) -> (h d) a", a=1), g_in),
                                (gcol[:, 1:2], gate_r.rearrange("h (d a) -> (h d) a", a=1), g_in),
                                (wgk_s[:, 0:LD], wgk, wg_in), (wgv_s[:], wgv, wg_in),
                                (rout_s[0:LD, :], r_out_w, wo_in), (wout_s[:], w_out, wo_in)):
                sp.dma_start(dst, src).then_inc(s, 16)
            load_x(1)
            sp.dma_start(b1r[:], b1.rearrange("e (c p) -> (e c) p", p=P)).then_inc(b_in, 16)
            for b in range(2, NB):
                load_x(b)
            sp.wait_ge(pad_ok, 1)
            sp.dma_start(seg.rearrange("(e s) w -> s e w", e=E)[0:P, :, :],
                         padrows[:].unsqueeze(1).to_broadcast([P, E, XW])).then_inc(padded, 16)
            for b in range(NB):
                sp.wait_ge(x_in[b], 16)
            sp.dma_start(b2r[:].rearrange("p e d -> p (e d)"),
                         b2.rearrange("e d -> (e d)").partition_broadcast(P)).then_inc(b2_in, 16)
            sp.dma_start(w1_s[:], W1.rearrange("e p f -> p e f")).then_inc(f_in, 16)
            sp.dma_start(w2_s[:], W2.rearrange("e (c p) d -> p e c d", p=P)).then_inc(f_in, 16)

            tail = load_table(sp, tail_table, [0], tails_ok, E * SEG - P)
            first = [0] + load_table(sp, tile_table, [1], table_ok, T + E)
            sp.wait_ge(scattered, 16 * T)

            def load(row, k):
                sp.dma_start(xs[:], seg[bass.ds(row, P), :]).then_inc(tile_in, 16)
                sp.dma_start(xk[:, bass.ds((k % RING) * XW, XW)], seg[bass.ds(row, P), :]).then_inc(kept, 16)

            for e in range(E):
                if e > 0:
                    tail += load_table(sp, tail_table, [e], tails_ok, E * SEG - P)
                    first += load_table(sp, tile_table, [e + 1], table_ok, T + E)
                with sp.Fori(first[e], first[e + 1]) as k:
                    sp.wait_ge(xT_up, k + 1)
                    sp.wait_ge(idx_ok, k + 1)
                    i = nc.s_assert_within(k - first[e], 0, T - 1,
                                           skip_runtime_bounds_check_because="a group has at most all T tiles")
                    load(nc.s_assert_within(tail[e] - i * P, 0, E * SEG - P,
                                            skip_runtime_bounds_check_because="rows of no token precede a group's"), k)
            sp.wait_ge(xT_up, first[E] + 1)
            sp.dma_start(xs[:], seg[(E - 1) * SEG:(E - 1) * SEG + P, :]).then_inc(tile_in, 16)

        @block.gpsimd
        def _(pool):
            count = [0]

            def link(ins):
                count[0] += 1
                ins.then_inc(pool_step, 1)
                pool.wait_ge(pool_step, count[0])

            def keep(v, base, pattern, mult, fill=0.0):
                link(nc.gpsimd.affine_select(out=v, in_=v, compare_op=ALU.is_ge, fill=fill, base=base,
                                             pattern=pattern, channel_multiplier=mult))

            link(nc.gpsimd.memset(ident[:], 0.0))
            nc.gpsimd.affine_select(out=ident[:], in_=ident[:], compare_op=ALU.not_equal, fill=1.0, base=0,
                                    pattern=[[-1, P]], channel_multiplier=1).then_inc(ident_ok, 1)
            nc.gpsimd.memset(half[:, 0:1], -0.5)
            nc.gpsimd.memset(half[:, 1:2], EPS)
            nc.gpsimd.memset(group4[:], 1.0)
            link(nc.gpsimd.memset(blk16[:], 1.0))
            keep(blk16[:], 0, [[-HD, H]], 1)
            keep(blk16[:], HD - 1, [[HD, H]], -1)
            link(nc.gpsimd.tensor_tensor(slot4[:], blk16[:, 0:4], blk16[:, 4:8], ALU.add))
            link(nc.gpsimd.tensor_tensor(slot4[:], slot4[:], blk16[:, 8:12], ALU.add))
            link(nc.gpsimd.tensor_tensor(slot4[:], slot4[:], blk16[:, 12:16], ALU.add))
            keep(group4[:], 0, [[-W, 4]], 1)
            nc.gpsimd.affine_select(out=group4[:], in_=group4[:], compare_op=ALU.is_ge, fill=0.0, base=W - 1,
                                    pattern=[[W, 4]], channel_multiplier=-1).then_inc(heads_ok, 1)
            nc.gpsimd.memset(sel_l[:], 0.0)
            link(nc.gpsimd.memset(neg_l[:], 0.0))
            link(nc.gpsimd.memset(neg_l[W:2 * W, 1, 0:W], NEG))
            v = sel_l[0:W, :].rearrange("r (n q) -> r n q", q=W)
            link(nc.gpsimd.affine_select(out=v, in_=v, compare_op=ALU.not_equal, fill=1.0, base=0,
                                         pattern=[[0, BLK], [-1, W]], channel_multiplier=1))
            v = sel_l[W:2 * W, 0:W]
            link(nc.gpsimd.affine_select(out=v, in_=v, compare_op=ALU.not_equal, fill=1.0, base=0,
                                         pattern=[[-1, W]], channel_multiplier=1))
            keep(neg_l[0:W, :, :], -1, [[0, 2], [1, 2 * W]], -1, NEG)
            nc.gpsimd.affine_select(out=neg_l[0:W, :, :], in_=neg_l[0:W, :, :], compare_op=ALU.is_ge, fill=NEG, base=W,
                                    pattern=[[0, 2], [-1, 2 * W]], channel_multiplier=1).then_inc(masks_ok, 1)

            def latent_masks():
                nc.gpsimd.memset(neg_r[:], 0.0)
                link(nc.gpsimd.memset(sel_r[:], 0.0))
                link(nc.gpsimd.memset(sel_r[0:P // CH, :], 1.0))
                keep(sel_r[0:P // CH, :], 0, [[1, P]], -CH)
                keep(sel_r[0:P // CH, :], CH - 1, [[-1, P]], CH)
                nc.gpsimd.affine_select(
                    out=neg_r[0:P // CH, :, :], in_=neg_r[0:P // CH, :, :], compare_op=ALU.is_ge, fill=NEG, base=0,
                    pattern=[[P // CH, KT_], [-1, NL]], channel_multiplier=1).then_inc(masks_ok, 1)

            def routing_constants():
                nc.gpsimd.memset(ones[:], 1.0)
                link(nc.gpsimd.memset(before[:], 1.0))
                keep(before[:], -1, [[1, P]], -1)
                link(nc.gpsimd.memset(padrows[:], 0.0))
                nc.gpsimd.iota(padrows[:, D:XW].bitcast(I32), pattern=[[0, 1]], base=T * P,
                               channel_multiplier=0).then_inc(pad_ok, 1)
                link(nc.gpsimd.iota(eint[:, 0:E], pattern=[[SEG, E]], base=P, channel_multiplier=0))
                link(nc.gpsimd.iota(eint[:, E:], pattern=[[1, E]], base=-3 * E, channel_multiplier=0))
                link(nc.gpsimd.tensor_copy(efl[:], eint[:]))
                link(nc.gpsimd.tensor_copy(nextrow[:], efl[:, 0:E]))
                link(nc.gpsimd.iota(x1[:, :, D].bitcast(I32), pattern=[[P, T]], base=0, channel_multiplier=1))

            def gate_columns():
                pool.wait_ge(g_in, 32)
                for q in range(2):
                    nc.gpsimd.tensor_scalar(gmat[:, q * H:(q + 1) * H], blk16[:], gcol[:, q:q + 1], None,
                                            ALU.mult).then_inc(gmat_ok, 1)

            def expand_k(b):
                pool.wait_ge(pj_free, pj[("K", b)] + 1)
                expand(nc.gpsimd, Kx[:, b % 2, :, W:], KT[:, b % 2, :], slot4[:], 4).then_inc(kx_done, 1)

            def expand_q(b):
                pool.wait_ge(pj_free, pj[("Q", b)] + 1)
                expand(nc.gpsimd, Qg[:, b % 2, :, :], QT[:, b % 2, :], group4[:], 4).then_inc(qg_done, 1)

            def expand_gk(b):
                pool.wait_ge(pj_free, pj[("G", b)] + 1)
                expand(nc.gpsimd, GKx[:, b % 2, :, :], GKs[:, b % 2, :], blk16[:, 0:LH], LH).then_inc(gk_done, 1)

            def layernorm(t):
                q = t % 2
                pool.wait_ge(stats, t + 1)
                link(nc.gpsimd.tensor_scalar(rstd[:, q, :], mv[:, q, 1:2], EPS, None, ALU.add))
                ins = nc.gpsimd.tensor_tensor(rstd[:, q, :], rstd[:, q, :], half[:, 0:1], ALU.pow)
                if t == T - 1:
                    ins.then_inc(rstd_ok, 1)
                    return
                link(ins)
                nc.gpsimd.tensor_scalar(x1[:, t, 0:D], y[:, q, :], mv[:, q, 0:1], rstd[:, q, :],
                                        ALU.subtract, ALU.mult).then_inc(ln_done, 1)

            def scatter(c):
                pool.wait_ge(placed, c + 1)
                if c == 0:
                    pool.wait_ge(padded, 16)
                for t in chunks[c]:
                    pool.wait_ge(ln_done, t + 1)
                    nc.gpsimd.indirect_dma_start(seg, bass.IndirectOffsetOnAxis(ap=pos[:, t:t + 1], axis=0),
                                                 x1[:, t, :], None).then_inc(scattered, 16)

            pool.wait_ge(pj_free, pj[("Q", 0)] + 1)
            expand(nc.gpsimd, Qg[:, 0, :, 0:P], QT[:, 0, 0:P], group4[:], 4).then_inc(qg_done, 1)
            latent_masks()
            gate_columns()
            expand_gk(0)
            expand(nc.gpsimd, Qg[:, 0, :, P:], QT[:, 0, P:], group4[:], 4).then_inc(qg_done, 1)
            routing_constants()
            for t in range(T + 3):
                b, k = divmod(t, KT_)
                if t >= 3:
                    layernorm(t - 3)
                if b + 1 < NB and k < 3:
                    (expand_k, expand_q, expand_gk)[k](b + 1)
                if t == 1:
                    pool.wait_ge(b2_in, 16)
                    nc.gpsimd.tensor_tensor(b2s[:, 0:E - 1, :], b2r[:, 0:E - 1, :], b2r[:, 1:E, :],
                                            ALU.add).then_inc(b2_ok, 1)
                    nc.gpsimd.tensor_tensor(b2s[:, E - 1, :], b2r[:, E - 1, :], b2r[:, 0, :], ALU.add).then_inc(b2_ok, 1)
                if k == 0 and 2 <= b <= NB:
                    scatter(b - 2)
            scatter(NB - 1)
            scatter(NB)

            ahead(pool, idx_ok, rs1, rs2, by=RING)
            first = [0] + load_table(pool, tile_table, range(1, E + 1), table_ok, T + E)

            def store(rows):
                nc.gpsimd.indirect_dma_start(
                    out.rearrange("b s d -> (b s) d"), bass.IndirectOffsetOnAxis(ap=idx[:], axis=0), rows, None,
                    bounds_check=T * P - 1, oob_is_err=False).then_inc(out_in, 16)

            link(nc.gpsimd.tensor_copy(idx[:], padrows[:, D:XW].bitcast(U32)))
            store(padrows[:, 0:D])
            pool.wait_ge(out_in, 16)
            store(padrows[:, 0:D])
            for e in range(E):
                with pool.Fori(first[e], first[e + 1]) as k:
                    pool.wait_ge(bn2, k + 1)
                    nc.gpsimd.tensor_tensor(rstd2[:], mv2[:, 1:2], half[:, 1:2], ALU.add).then_inc(rs1, 1)
                    pool.wait_ge(rs1, k + 1 + RING)
                    nc.gpsimd.tensor_tensor(rstd2[:], rstd2[:], half[:, 0:1], ALU.pow).then_inc(rs2, 1)
                    pool.wait_ge(out_in, k * 16 + 32)
                    nc.gpsimd.tensor_copy(idx[:], xk[:, bass.ds((k % RING) * XW + D, 1)].bitcast(U32)).then_inc(idx_ok, 1)
                    pool.wait_ge(table_ok, 1)
                    pool.wait_ge(idx_ok, k + 1 + RING)
                    pool.wait_ge(yo_ok, k + 1 + RING)
                    store(yo[:])
            pool.wait_ge(table_ok, 1)
            pool.wait_ge(out_in, first[E] * 16 + 32)

        @block.scalar
        def _(act):
            act.dma_start(wk_s[:], wk).then_inc(wk_in, 16)
            act.dma_start(wq_s[:], wq).then_inc(wq_in, 16)

            def take(use):
                kind, n = use
                act.wait_ge(pj_ready, pj[use] + 1)
                q = n % 2
                src = early_bank.get(use, bJ)
                if kind == "xT":
                    i = nc.scalar.copy(xT[:, q, W:], src[:])
                elif kind == "K":
                    i = nc.scalar.copy(KT[:, q, :], src[:])
                elif kind == "Q":
                    i = nc.scalar.copy(QT[:, q, :], src[:])
                elif kind == "GQ":
                    i = nc.scalar.copy(GQT[:, q, :], src[:])
                elif kind == "B":
                    i = nc.scalar.copy(b1c[:], bJ[:, 0:E * FC])
                elif kind == "R":
                    if n >= 1:
                        act.wait_ge(placed, n)
                    m = (len(chunks[n]) + 1) * E
                    i = nc.scalar.copy(ranks[:].rearrange("p k e -> p (k e)")[:, 0:m], bJ[:, 0:m])
                elif kind == "V":
                    if n >= 2:
                        act.wait_ge(pv_done, 3 * (n - 1))
                    for c in range(2):
                        h = slice(64 * c, 64 * c + 64)
                        i = nc.scalar.copy(Vx[h, q, :, :, c * HD:(c + 1) * HD],
                                           bJ[h, 0:BLK * D // 2].rearrange("p (n a d) -> p n a d", n=BLK, d=HD))
                else:
                    nc.scalar.mul(GKs[:, q, :], src[:, 0:NL], 1.0 / CH)
                    for c in range(2):
                        h = slice(64 * c, 64 * c + 64)
                        nc.scalar.mul(GVx[h, q, :, c * HD:(c + 1) * HD],
                                      src[h, NL:NL + LD // 2].rearrange("p (a d) -> p a d", d=HD),
                                      1.0 / CH)
                    i = nc.scalar.activation(gex[:, q, :, :],
                                             src[:, P:P + KT_ * 2 * H].rearrange("p (k g) -> p k g", k=KT_),
                                             ACT.Exp, scale=-1.0)
                i.then_inc(pj_free, 1)

            def exp(t, j):
                act.wait_ge(shifted, 3 * t + j + 1)
                v = Pr[:, t % 2, j, :]
                nc.scalar.activation(v, v, ACT.Exp, scale=SCALE).then_inc(exped, 1)

            def turned_copy(t, j):
                u = 3 * t + j
                act.wait_ge(turned, u + 1)
                if t >= 1:
                    act.wait_ge(pv_done, u - 2)
                nc.scalar.copy(PTs[:, j, :, :], bT[u % 2][:].rearrange("p (c q) -> p c q", c=4)).then_inc(turned_out, 1)

            act.wait_ge(ident_ok, 1)
            nc.scalar.activation(warm[:], ident[0:1, 0:1], ACT.Exp)
            act.wait_ge(vconst_ok, 1)
            for use in first_uses:
                take(use)
            for t in range(T + 3):
                for j in range(2):
                    if 1 <= t <= T:
                        turned_copy(t - 1, j)
                if t >= 3:
                    act.wait_ge(attT_up, t - 2)
                    nc.scalar.copy(attT[:], aT).then_inc(attT_out, 1)
                if t < T:
                    take(("V", t))
                    for use in early_uses if t == 0 else []:
                        take(use)
                    exp(t, 0)
                if 1 <= t <= T:
                    turned_copy(t - 1, 2)
                if t < T:
                    exp(t, 1)
                if 2 <= t < T + 2:
                    act.wait_ge(remT_up, t - 1)
                    nc.scalar.copy(remT[:], rT).then_inc(remT_out, 1)
                for use in others(t):
                    take(use)
                if t < T:
                    exp(t, 2)
            take(("R", NB))

            ahead(act, relu_a)
            first = [0] + load_table(act, tile_table, range(1, E + 1), table_ok, T + E)
            for e in range(E):
                a = (e + 1) % E
                with act.Fori(first[e], first[e + 1]) as k:
                    act.wait_ge(up_a, k + 1)
                    act.wait_ge(down, k + 1)
                    for c in range(FC):
                        nc.scalar.activation(ha[:, c, :], bA[:, c * P:(c + 1) * P], ACT.Relu,
                                             bias=b1c[:, e * FC + c:e * FC + c + 1]).then_inc(relu_a, 1)
                    act.wait_ge(up_b, k + 2)
                    for c in range(BA):
                        nc.scalar.activation(hb[:, c, :], bB[:, c * P:(c + 1) * P], ACT.Relu,
                                             bias=b1c[:, a * FC + c:a * FC + c + 1]).then_inc(relu_a, 1)

        @block.vector
        def _(dve):
            count = [0]

            def link(ins):
                count[0] += 1
                ins.then_inc(dve_step, 1)
                dve.wait_ge(dve_step, count[0])

            nc.vector.memset(xT[:, :, 0:W], 0.0)
            nc.vector.memset(Kx[:, :, :, 0:W], 0.0)
            for v in (wgq_s[:, LD:], wgk_s[:, LD:], rout_s[LD:, :], rem[:, :, LD:], GVx[:]):
                nc.vector.memset(v, 0.0)
            nc.vector.memset(tiles[:], 0.0)
            link(nc.vector.memset(Vx[:], 0.0))
            for c in range(2):
                h = slice(64 * c, 64 * c + 64)
                nc.vector.memset(Vx[h, :, :, :, 2 * HD + c:2 * HD + c + 1], 1.0)
                last = nc.vector.memset(GVx[h, :, :, 2 * HD + c:2 * HD + c + 1], 1.0)
            last.then_inc(vconst_ok, 1)

            def pooled(b):
                dve.wait_ge(pj_free, pj[("xT", b)] + 1)
                nc.vector.tensor_reduce(xp[:, b % 2, :], xT[:, b % 2, W:].rearrange("p (n c) -> p n c", c=CH),
                                        AX.X, ALU.add).then_inc(xp_done, 1)

            def gates(b):
                dve.wait_ge(pj_free, pj[("G", b)] + 1)
                g = gat[:, b % 2, :, :]
                link(nc.vector.tensor_scalar(g, gex[:, b % 2, :, :], 1.0, None, ALU.add))
                link(nc.vector.reciprocal(g, g))

            def shift(t, j):
                u = 3 * t + j
                dve.wait_ge(scores, u + 1)
                s = bS[j][:].rearrange("p (h k) -> p h k", h=8)
                link(nc.vector.tensor_reduce(mx[:, j, :], s, AX.X, ALU.max))
                if t >= 2:
                    dve.wait_ge(turned, u - 5)
                nc.vector.tensor_tensor(Pr[:, t % 2, j, :].rearrange("p (h k) -> p h k", h=8), s,
                                        mx[:, j, :].unsqueeze(2).to_broadcast([P, 8, 2 * W]),
                                        ALU.subtract).then_inc(shifted, 1)

            def normalise(t):
                q, b, k = t % 2, t // KT_, t % KT_
                dve.wait_ge(pv_done, 3 * t + 3)
                pv = bV[:, 0:(HP + LP) * PW].rearrange("p (a c) -> p a c", c=PW)
                link(nc.vector.reciprocal(rs[:, q, :, :], pv[:, :, 2 * HD:]))
                link(nc.vector.tensor_tensor(grs[:, q, :], rs[:, q, 0:HP, :].rearrange("p a c -> p (a c)"),
                                             gat[:, b % 2, k, 0:H], ALU.mult))
                nc.vector.tensor_tensor(
                    loc[:, q, :].rearrange("p (a c d) -> p a c d", c=2, d=HD),
                    pv[:, 0:HP, 0:2 * HD].rearrange("p a (c d) -> p a c d", c=2),
                    grs[:, q, :].rearrange("p (a c) -> p a c", c=2).unsqueeze(3).to_broadcast([P, HP, 2, HD]), ALU.mult)
                nc.vector.tensor_tensor(
                    rem[:, q, 0:LD].rearrange("p (a c d) -> p a c d", c=2, d=HD),
                    pv[:, HP:, 0:2 * HD].rearrange("p a (c d) -> p a c d", c=2),
                    rs[:, q, HP:, :].unsqueeze(3).to_broadcast([P, LP, 2, HD]), ALU.mult).then_inc(normed, 1)

            def gate(t):
                q, b, k = t % 2, t // KT_, t % KT_
                dve.wait_ge(rem_up, t + 1)
                if t >= 1:
                    dve.wait_ge(attT_up, t)
                link(nc.vector.tensor_tensor(
                    att0[:].rearrange("p (h d) -> p h d", d=HD), rM.rearrange("p (h d) -> p h d", d=HD),
                    gat[:, b % 2, k, H:].unsqueeze(2).to_broadcast([P, H, HD]), ALU.mult))
                nc.vector.tensor_tensor(att[:], att0[:], loc[:, q, :], ALU.add).then_inc(gated, 1)

            def residual(t):
                q = t % 2
                dve.wait_ge(proj_up, t + 1)
                if t >= 2:
                    dve.wait_ge(ln_done, t - 1)
                ins = nc.vector.tensor_tensor(y[:, q, :], wO, x_tok[:, t, :], ALU.add)
                ins.then_inc(summed, 1)
                dve.wait_ge(summed, t + 1)
                link(nc.vector.bn_stats(st[:, q, :], y[:, q, :]))
                nc.vector.bn_aggr(mv[:, q, :], st[:, q, :]).then_inc(stats, 1)

            def mark_rounded(c):
                m = len(chunks[c])
                dve.wait_ge(ln_done, chunks[c].stop)
                v = x1[:, chunks[c].start:chunks[c].stop, :]
                link(nc.vector.tensor_tensor(tsum[:, 0:m], v[:, :, 0], v[:, :, 1], ALU.add))
                link(nc.vector.tensor_scalar(near[:, 0:m], tsum[:, 0:m], ROUND, -ROUND, ALU.add, ALU.add))
                link(nc.vector.tensor_tensor(off[:, 0:m], near[:, 0:m], tsum[:, 0:m], ALU.subtract))

            def mark_truncated(c):
                m = len(chunks[c])
                nc.vector.tensor_scalar(over[:, 0:m], off[:, 0:m], 0.0, None, ALU.is_gt)
                link(nc.vector.tensor_scalar(frac[:, 0:m], off[:, 0:m], 0.0, None, ALU.not_equal))
                link(nc.vector.tensor_tensor(near[:, 0:m], near[:, 0:m], over[:, 0:m], ALU.subtract))
                link(nc.vector.scalar_tensor_tensor(frac[:, 0:m], tsum[:, 0:m], 0.0, frac[:, 0:m], ALU.is_lt, ALU.mult))
                link(nc.vector.tensor_tensor(near[:, 0:m], near[:, 0:m], frac[:, 0:m], ALU.add))

            def mark_group(c):
                m = len(chunks[c])
                link(nc.vector.tensor_scalar(off[:, 0:m], near[:, 0:m], 1.0 / E, 3.0 - 0.5 + 0.5 / E, ALU.mult, ALU.add))
                link(nc.vector.tensor_scalar(off[:, 0:m], off[:, 0:m], ROUND, -ROUND, ALU.add, ALU.add))
                link(nc.vector.scalar_tensor_tensor(near[:, 0:m], off[:, 0:m], -float(E), near[:, 0:m],
                                                    ALU.mult, ALU.add))
                nc.vector.tensor_tensor(onehot[:, 0:m, :], near[:, 0:m].unsqueeze(2).to_broadcast([P, m, E]),
                                        efl[:, E:].unsqueeze(1).to_broadcast([P, m, E]),
                                        ALU.is_equal).then_inc(marked, 1)

            def mark(c):
                mark_rounded(c)
                mark_truncated(c)
                mark_group(c)

            def place(c):
                m = len(chunks[c])
                dve.wait_ge(marked, c + 1)
                dve.wait_ge(pj_free, pj[("R", c)] + 1)
                link(nc.vector.tensor_tensor(cand[:, 0:m, :], ranks[:, 0:m, :],
                                             nextrow[:].unsqueeze(1).to_broadcast([P, m, E]), ALU.add))
                link(nc.vector.tensor_tensor(cand[:, 0:m, :], cand[:, 0:m, :], onehot[:, 0:m, :], ALU.mult))
                link(nc.vector.tensor_reduce(posf[:, 0:m], cand[:, 0:m, :], AX.X, ALU.add))
                link(nc.vector.tensor_tensor(nextrow[:], nextrow[:], ranks[:, m, :], ALU.add))
                nc.vector.tensor_copy(pos[:, chunks[c].start:chunks[c].stop], posf[:, 0:m]).then_inc(placed, 1)

            def count_tiles():
                link(nc.vector.tensor_scalar(tiles[:, 3, 0:E], nextrow[0:1, :], -float(P), None, ALU.add))
                nc.vector.tensor_copy(tail_table[:], tiles[:, 3, 0:E]).then_inc(tails_ok, 1)
                n, m = tiles[:, 0, :], tiles[:, 1, :]
                link(nc.vector.tensor_tensor(m[:, Z + 1:], nextrow[0:1, :], efl[0:1, 0:E], ALU.subtract))
                link(nc.vector.tensor_scalar(m[:, Z + 1:], m[:, Z + 1:], 1.0 / P, 0.5 - 0.5 / P, ALU.mult, ALU.add))
                link(nc.vector.tensor_scalar(m[:, Z + 1:], m[:, Z + 1:], ROUND, -ROUND, ALU.add, ALU.add))
                link(nc.vector.tensor_scalar(n[:, Z + 1:], m[:, Z + 1:], 1.0, None, ALU.max))
                src, dst, d = n, m, 1
                while d <= E:
                    link(nc.vector.tensor_tensor(dst[:, Z:], src[:, Z:], src[:, Z - d:Z + E + 1 - d], ALU.add))
                    src, dst, d = dst, (tiles[:, 2, :] if dst is m else m), 2 * d
                nc.vector.tensor_copy(tile_table[:], src[:, Z:]).then_inc(table_ok, 1)

            pooled(0)
            dve.wait_ge(pj_free, pj[("K", 0)] + 1)
            dve.wait_ge(heads_ok, 1)
            for o in (slice(0, P), slice(P, S)):
                expand(nc.vector, Kx[:, 0, :, W + o.start:W + o.stop], KT[:, 0, o], slot4[:], 4).then_inc(kx_done, 1)
            for t in range(T + 3):
                b, k = divmod(t, KT_)
                if 2 <= t < T + 2:
                    normalise(t - 2)
                if t < T:
                    shift(t, 0)
                    if k == 1 and b + 1 < NB:
                        pooled(b + 1)
                    if k == 3 and 1 <= b < NB:
                        mark_rounded(b - 1)
                    shift(t, 1)
                    if k == 3 and 1 <= b < NB:
                        mark_truncated(b - 1)
                    if k == 0:
                        gates(b)
                if k == 0 and 2 <= b <= NB:
                    mark_group(b - 2)
                if t >= 3:
                    residual(t - 3)
                if t < T:
                    shift(t, 2)
                if 2 <= t < T + 2:
                    gate(t - 2)
                if t == T + 1:
                    mark(NB - 1)
                if k == 0 and 2 <= b <= NB:
                    place(b - 2)
            place(NB - 1)
            dve.wait_ge(rstd_ok, 1)
            q = (T - 1) % 2
            nc.vector.tensor_scalar(x1[:, T - 1, 0:D], y[:, q, :], mv[:, q, 0:1], rstd[:, q, :],
                                    ALU.subtract, ALU.mult).then_inc(ln_done, 1)
            mark(NB)
            place(NB)
            count_tiles()

            dve.wait_ge(b2_ok, 2)
            ahead(dve, xT_out, relu_b, biased, y_ok)
            ahead(dve, yo_ok, by=RING - 1)
            for v in (y2[:], mv2[:], rstd2[:]):
                link(nc.vector.memset(v, 0.0))
            first = [0] + load_table(dve, tile_table, range(1, E + 1), table_ok, T + E)

            def column_copy(k):
                dve.wait_ge(xT_up, k + 2)
                dve.wait_ge(up_b, k + 1)
                nc.vector.tensor_copy(xsT[:], bX[:, 0:P]).then_inc(xT_out, 1)

            def finish(k):
                dve.wait_ge(rs2, k + RING)
                dve.wait_ge(out_in, k * 16 + 16)
                nc.vector.tensor_scalar(yo[:], y2[:], mv2[:, 0:1], rstd2[:, 0:1],
                                        ALU.subtract, ALU.mult).then_inc(yo_ok, 1)

            column_copy(0)
            for e in range(E):
                a = (e + 1) % E
                with dve.Fori(first[e], first[e + 1]) as k:
                    dve.wait_ge(up_b, k + 2)
                    dve.wait_ge(down, k + 1)
                    for c in range(BA, FC):
                        nc.vector.tensor_scalar(hb[:, c, :], bC[:, c * P:(c + 1) * P], b1c[:, a * FC + c:a * FC + c + 1],
                                                0.0, ALU.add, ALU.max).then_inc(relu_b, 1)
                    column_copy(k + 1)
                    finish(k)
                    dve.wait_ge(down, k + 2)
                    nc.vector.tensor_tensor(ysum[:], bY[:, 0:D], b2s[:, e, :], ALU.add).then_inc(biased, 1)
                    dve.wait_ge(biased, k + 2)
                    dve.wait_ge(kept, k * 16 + 16)
                    nc.vector.scalar_tensor_tensor(y2[:], ysum[:], 0.5, xk[:, bass.ds((k % RING) * XW, D)],
                                                   ALU.mult, ALU.add).then_inc(y_ok, 1)
                    dve.wait_ge(y_ok, k + 2)
                    nc.vector.bn_stats(st2[:], y2[:]).then_inc(bn1, 1)
                    dve.wait_ge(table_ok, 1)
                    dve.wait_ge(bn1, k + 1)
                    nc.vector.bn_aggr(mv2[:], st2[:]).then_inc(bn2, 1)
            finish(first[E])

        @block.tensor
        def _(pe):
            mm = nc.tensor.matmul

            def half_heads(w, c):
                return w[:].rearrange("p (a c d) -> p a c d", c=2, d=HD)[:, :, c, :]

            def fill(use):
                kind, n = use
                if use in early_bank:
                    pe.wait_ge(pj_free, pj[("xT", 0)] + 1)
                elif use == ("V", 0):
                    pe.wait_ge(pj_free, pj[("xT", 0)] + 1)
                elif pj[use] >= 1:
                    pe.wait_ge(pj_free, pj[use])
                q = n % 2
                dst = early_bank.get(use, bJ)
                if kind == "xT":
                    pe.wait_ge(x_in[n], 16)
                    for i in range(KT_):
                        last = nc.tensor.transpose(bJ[:, i * P:(i + 1) * P], x_tok[:, n * KT_ + i, :], ident[:])
                elif kind == "K":
                    if n == 0:
                        pe.wait_ge(wk_in, 16)
                    last = mm(dst[:], wk_s[:], xT[:, q, W:], start=True, stop=True)
                elif kind == "Q":
                    if n == 0:
                        pe.wait_ge(wq_in, 16)
                    last = mm(dst[:], wq_s[:], xT[:, q, W:], start=True, stop=True)
                elif kind == "GQ":
                    if n == 0:
                        pe.wait_ge(wgq_in, 16)
                    last = mm(dst[:], wgq_s[:], xT[:, q, W:], start=True, stop=True)
                elif kind == "B":
                    pe.wait_ge(b_in, 16)
                    last = nc.tensor.transpose(bJ[:, 0:E * FC], b1r[:], ident[0:E * FC, 0:E * FC])
                elif kind == "R":
                    pe.wait_ge(marked, n + 1)
                    m = len(chunks[n])
                    oh = onehot[:].rearrange("p k e -> p (k e)")
                    mm(bJ[:, 0:m * E], before[:], oh[:, 0:m * E], start=True, stop=False, skip_group_check=True)
                    for i in range(1, m + 1):
                        last = mm(bJ[:, i * E:(m + 1) * E], ones[:], oh[:, 0:(m + 1 - i) * E], start=False,
                                  stop=(i == m), skip_group_check=True)
                elif kind == "G":
                    pe.wait_ge(xp_done, n + 1)
                    if n == 0:
                        pe.wait_ge(wg_in, 32)
                        pe.wait_ge(gmat_ok, 2)
                        pe.wait_ge(pj_free, pj[("Q", 0)] + 1)
                    mm(dst[:, 0:NL], wgk_s[:], xp[:, q, :], start=True, stop=True)
                    for r in range(BLK):
                        mm(dst[r * W:(r + 1) * W, NL:NL + LD // 2], xp[:, q, (r % 2) * W:(r % 2 + 1) * W],
                           half_heads(wgv_s, r // 2), start=True, stop=True)
                    for i in range(KT_):
                        last = mm(dst[:, P + i * 2 * H:P + (i + 1) * 2 * H], QT[:, q, i * P:(i + 1) * P], gmat[:],
                                  start=True, stop=True)
                else:
                    b, k = divmod(n, KT_)
                    for i in range(BLK):
                        o = k * P + i * W
                        for r in range(BLK):
                            w = o + (r % 2) * W
                            last = mm(bJ[r * W:(r + 1) * W, i * D // 2:(i + 1) * D // 2], xT[:, b % 2, w:w + W],
                                      half_heads(wv_s, r // 2), start=True, stop=True)
                last.then_inc(pj_ready, 1)

            def mask(t, j):
                if t == 0 and j != 1:
                    pe.wait_ge(masks_ok, 1 + j // 2)
                if t >= 1:
                    pe.wait_ge(shifted, 3 * t + j - 2)
                k = t % KT_
                if j < 2:
                    sel, neg = sel_l, neg_l[:, 1 if k == 0 else 0, :]
                else:
                    sel, neg = sel_r, neg_r[:, k, :]
                mm(bS[j][:], sel[:], neg.unsqueeze(1).to_broadcast([P, 8, 2 * W]),
                   start=True, stop=False, skip_group_check=True)

            def score_local(t, j):
                b, k = divmod(t, KT_)
                q = b % 2
                if t <= 1 and j == 0:
                    pe.wait_ge(kx_done, t + 1)
                    pe.wait_ge(qg_done, t + 1)
                elif k == 0 and j == 0:
                    pe.wait_ge(kx_done, b + 2)
                    pe.wait_ge(qg_done, b + 2)
                for g in range(2):
                    for i in range(BLK):
                        o = k * P + i * W
                        last = mm(bS[j][i * W:(i + 1) * W, g * 256:(g + 1) * 256],
                                  Qg[:, q, 2 * j + g, o:o + W], Kx[:, q, :, o:o + 2 * W],
                                  start=False, stop=(g == 1), skip_group_check=True)
                last.then_inc(scores, 1)

            def score_latent(t):
                b, k = divmod(t, KT_)
                if k == 0:
                    pe.wait_ge(gk_done, b + 1)
                mm(bS[2][:], GQT[:, b % 2, k * P:(k + 1) * P], GKx[:, b % 2, :, :].rearrange("p h n -> p (h n)"),
                   start=False, stop=True, skip_group_check=True).then_inc(scores, 1)

            def turn(t, j):
                u = 3 * t + j
                pe.wait_ge(exped, u + 1)
                if u >= 2:
                    pe.wait_ge(turned_out, u - 1)
                for c in range(4):
                    last = nc.tensor.transpose(bT[u % 2][:, c * P:(c + 1) * P], Pr[:, t % 2, j, c * P:(c + 1) * P], ident[:])
                last.then_inc(turned, 1)

            def weigh(t, j):
                u, q = 3 * t + j, t % 2
                pe.wait_ge(turned_out, u + 1)
                if j == 0:
                    pe.wait_ge(pj_free, pj[("V", t)] + 1)
                    if t >= 1:
                        pe.wait_ge(normed, t)
                for c in range(4):
                    a = 4 * j + c
                    if j < 2:
                        for i in range(BLK):
                            last = mm(bV[i * W:(i + 1) * W, a * PW:(a + 1) * PW], PTs[:, j, c, i * W:(i + 1) * W],
                                      Vx[:, q, i, a, :], start=True, stop=True)
                    else:
                        last = mm(bV[:, a * PW:(a + 1) * PW], PTs[:, j, c, :], GVx[:, (t // KT_) % 2, c, :],
                                  start=True, stop=True)
                last.then_inc(pv_done, 1)

            pe.wait_ge(ident_ok, 1)
            pe.wait_ge(vconst_ok, 1)
            for use in first_uses:
                fill(use)
            for t in range(T + 3):
                for j in range(2):
                    if t < T:
                        mask(t, j)
                    if 1 <= t <= T:
                        turn(t - 1, j)
                if t >= 3:
                    pe.wait_ge(gated, t - 2)
                    nc.tensor.transpose(aT, att[:], ident[:]).then_inc(attT_up, 1)
                if t < T:
                    if t == 0:
                        pe.wait_ge(wv_in, 16)
                    fill(("V", t))
                    score_local(t, 0)
                    score_local(t, 1)
                    for use in early_uses if t == 0 else []:
                        fill(use)
                if 1 <= t <= T:
                    weigh(t - 1, 0)
                    weigh(t - 1, 1)
                if t >= 3:
                    pe.wait_ge(attT_out, t - 2)
                    mm(wO, attT[:], wout_s[:], start=True, stop=True).then_inc(proj_up, 1)
                if 1 <= t <= T:
                    turn(t - 1, 2)
                if t < T:
                    mask(t, 2)
                    score_latent(t)
                if 2 <= t < T + 2:
                    pe.wait_ge(normed, t - 1)
                    if t >= 3:
                        pe.wait_ge(summed, t - 2)
                    nc.tensor.transpose(rT, rem[:, t % 2, :], ident[:]).then_inc(remT_up, 1)
                for use in others(t)[0:1]:
                    fill(use)
                if 1 <= t <= T:
                    weigh(t - 1, 2)
                if 2 <= t < T + 2:
                    if t == 2:
                        pe.wait_ge(wo_in, 32)
                    pe.wait_ge(remT_out, t - 1)
                    mm(rM, remT[:], rout_s[:], start=True, stop=True).then_inc(rem_up, 1)
                for use in others(t)[1:]:
                    fill(use)
            fill(("R", NB))

            pe.wait_ge(f_in, 32)
            ahead(pe, xT_up, up_b, down)
            first = [0] + load_table(pe, tile_table, range(1, E + 1), table_ok, T + E)

            def columns(k):
                pe.wait_ge(tile_in, (k + 1) * 16)
                pe.wait_ge(xT_out, k + 1)
                nc.tensor.transpose(bX[:, 0:P], xs[:, 0:D], ident[:]).then_inc(xT_up, 1)

            columns(0)
            for e in range(E):
                a = (e + 1) % E
                with pe.Fori(first[e], first[e + 1]) as k:
                    pe.wait_ge(xT_out, k + 2)
                    pe.wait_ge(relu_a, k * (FC + BA) + 1)
                    for c in range(FC):
                        last = mm(bA[:, c * P:(c + 1) * P], w1_s[:, e, c * P:(c + 1) * P], xsT[:], start=True, stop=True)
                    last.then_inc(up_a, 1)
                    pe.wait_ge(relu_b, k * (FC - BA) + 1)
                    for c in range(FC):
                        last = mm((bB if c < BA else bC)[:, c * P:(c + 1) * P], w1_s[:, a, c * P:(c + 1) * P], xsT[:], start=True, stop=True)
                    last.then_inc(up_b, 1)
                    pe.wait_ge(biased, k + 1)
                    for c in range(FC):
                        pe.wait_ge(relu_a, k * (FC + BA) + c + 2)
                        mm(bY[:, 0:D], ha[:, c, :], w2_s[:, e, c, :], start=(c == 0), stop=False)
                    columns(k + 1)
                    for c in range(FC):
                        if c < BA:
                            pe.wait_ge(relu_a, k * (FC + BA) + FC + c + 2)
                        else:
                            pe.wait_ge(relu_b, k * (FC - BA) + c - BA + 2)
                        last = mm(bY[:, 0:D], hb[:, c, :], w2_s[:, a, c, :], start=False, stop=(c == FC - 1))
                    last.then_inc(down, 1)


_INS = ["L0_attn_x", "L0_attn_wq", "L0_attn_wk", "L0_attn_wv", "L0_attn_wgq", "L0_attn_wgk", "L0_attn_wgv",
        "L0_attn_r_out_w", "L0_attn_gate_local_w", "L0_attn_gate_remote_w", "L0_attn_w_out",
        "L0_ffn_W1", "L0_ffn_b1", "L0_ffn_W2", "L0_ffn_b2"]


def kernel(**inputs):
    import numpy as _np
    import concourse.bacc as _bacc
    from concourse import mybir as _mybir
    from concourse.bass_utils import run_bass_kernel_spmd as _run

    nc = _bacc.Bacc("TRN2", target_bir_lowering=False, num_devices=1)
    arrays, args = {}, []
    for name in _INS:
        a = _np.ascontiguousarray(inputs[name])
        arrays[f"in_{name}"] = a
        args.append(nc.dram_tensor(f"in_{name}", a.shape, _mybir.dt.from_np(a.dtype), kind="ExternalInput").ap())
    shape = inputs["L0_attn_x"].shape
    args.append(nc.dram_tensor("out0", shape, F32, kind="ExternalOutput").ap())
    n = shape[0] * shape[1]
    experts = inputs["L0_ffn_W1"].shape[0]
    args.append(nc.dram_tensor("groups", (experts * (n + P), P + 1), F32, kind="Internal").ap())
    bass_windowed_latent_attention_hash_moe(nc, *args)
    r = _run(nc, [arrays], core_ids=[0])
    return r.results[0]["out0"]
```
